# Optimizing a Trainium2 kernel written in Bass

```python
import numpy as np
import jax
import jax.numpy as jnp

def _softmax(x, axis=-1):
    return jax.nn.softmax(x, axis=axis)

def _gelu(x):
    return jax.nn.gelu(x, approximate=True)

def _silu(x):
    return jax.nn.silu(x)

def _sigmoid(x):
    return jax.nn.sigmoid(x)

def _layernorm(x, axis=-1, eps=1e-05):
    m = jnp.mean(x, axis=axis, keepdims=True)
    v = jnp.var(x, axis=axis, keepdims=True)
    return (x - m) / jnp.sqrt(v + eps)

def _scatter_add(tgt, idx, src, axis=0):
    return tgt.at[idx].add(src)

def _segment_sum(src, seg, n):
    return jax.ops.segment_sum(src, seg, n)
kernel_name = 'mk_adj_resnorm_d2_adj_r2_472b78'

def setup_inputs(seed: int=0):
    np.random.seed(seed)
    _w = jnp.asarray

    def _rec_inputs():
        import jax
        import jax.numpy as jnp
        _gk = jax.random.key(seed)
        x = -0.0001071 + 1.001 * jax.random.normal(jax.random.fold_in(_gk, 1), (8, 1500, 64), jnp.float32)
        _a = jax.random.bernoulli(jax.random.fold_in(_gk, 2), 0.00133333, (8, 1500, 1500))
        _af = _a.astype(jnp.float32)
        adj = _af
        return (x, adj)
    x, adj = _rec_inputs()

    def _L0_gnn_setup():
        import jax, jax.numpy as jnp
        import numpy as np
        B, N, F = (2, 1500, 64)
        H, OUT, ATT = (4, 16, 16)
        DENSITY = 0.01
        key = jax.random.key(seed)
        ks = jax.random.split(key, 6)
        h = jax.random.normal(ks[0], (B, N, F), dtype=jnp.float32)
        a = (jax.random.uniform(ks[1], (B, N, N)) < DENSITY).astype(jnp.float32)
        glorot = lambda k, shape: jax.random.uniform(k, shape, jnp.float32, -1.0, 1.0) * jnp.sqrt(6.0 / (shape[-2] + shape[-1]))
        kernel = glorot(ks[2], (H, F, OUT))
        attention_kernel = glorot(ks[3], (H, F, ATT))
        attention_kernel_2 = glorot(ks[4], (H, F, ATT))
        bias = jax.random.normal(ks[5], (1, 1, H, OUT), dtype=jnp.float32) * 0.01
        return {'h': h, 'a': a, 'kernel': kernel, 'attention_kernel': attention_kernel, 'attention_kernel_2': attention_kernel_2, 'bias': bias}
    _L0_gnn_all = _L0_gnn_setup()
    _L0_gnn_in = {k: v for k, v in _L0_gnn_all.items() if k in ('kernel', 'attention_kernel', 'attention_kernel_2', 'bias')}
    del _L0_gnn_all

    def _L1_gnn_setup():
        import jax, jax.numpy as jnp
        import numpy as np
        key = jax.random.key(seed)
        k1, k2 = jax.random.split(key)
        B, N, D = (8, 2048, 64)
        x = jax.random.normal(k1, (B, N, D), dtype=jnp.float32)
        A = jax.random.uniform(k2, (B, N, N), dtype=jnp.float32)
        return {'x': x, 'A': A}
    _L1_gnn_all = _L1_gnn_setup()
    _L1_gnn_in = {k: v for k, v in _L1_gnn_all.items() if k in ()}
    del _L1_gnn_all
    return {'x': x, 'adj': adj, 'L0_gnn_kernel': _L0_gnn_in['kernel'], 'L0_gnn_attention_kernel': _L0_gnn_in['attention_kernel'], 'L0_gnn_attention_kernel_2': _L0_gnn_in['attention_kernel_2'], 'L0_gnn_bias': _L0_gnn_in['bias']}

def reference(x, adj, L0_gnn_kernel, L0_gnn_attention_kernel, L0_gnn_attention_kernel_2, L0_gnn_bias):
    import jax
    import jax.numpy as jnp

    def _L0_gnn_ref(h, a, kernel, attention_kernel, attention_kernel_2, bias):
        import jax, jax.numpy as jnp
        import numpy as np
        B, N, F = (2, 1500, 64)
        H, OUT, ATT = (4, 16, 16)
        DENSITY = 0.01
        feats = jnp.einsum('bnf,hfo->bhno', h, kernel)
        f_self = jnp.einsum('bnf,hfd->hbnd', h, attention_kernel)
        f_other = jnp.einsum('bnf,hfd->hbdn', h, attention_kernel_2)
        a_h = a[None]
        scores = jnp.einsum('hbnd,hbdm->hbnm', f_self, f_other)
        masked = a_h * scores
        masked = jnp.where(masked >= 0, masked, 0.2 * masked)
        masked = masked / jnp.sqrt(jnp.float32(ATT))
        masked = masked + jnp.where(a_h == 0, jnp.float32(-1000000000.0), jnp.float32(0.0))
        attn = jax.nn.softmax(masked, axis=-1)
        attn = attn * jnp.where(a_h == 0, jnp.float32(0.0), jnp.float32(1.0))
        attn = jnp.transpose(attn, (1, 0, 2, 3))
        node_features = jnp.einsum('bhnm,bhmo->bhno', attn, feats)
        node_features = node_features + jnp.transpose(bias, (0, 2, 1, 3))
        node_features = jax.nn.relu(node_features)
        node_features = jnp.transpose(node_features, (0, 2, 1, 3))
        return node_features.reshape(-1, N, H * OUT)

    def _L1_gnn_ref(x, A):
        import jax, jax.numpy as jnp
        import numpy as np
        deg = jnp.clip(jnp.sum(A, axis=2, keepdims=True), 1.0, None)
        A_norm = A / deg
        messages = jnp.matmul(A_norm, x)
        return messages
    x = _layernorm(x + _L0_gnn_ref(x, adj, L0_gnn_kernel, L0_gnn_attention_kernel, L0_gnn_attention_kernel_2, L0_gnn_bias), axis=-1)
    x = _layernorm(x + _L1_gnn_ref(x, adj), axis=-1)
    return x

_drawn_inputs = setup_inputs


def setup_inputs(seed=0):
    import zlib

    import numpy as np

    out = dict(_drawn_inputs(seed))
    spreads = {}
    factors = {'L0_gnn_bias': 6.303}
    for name, (base, spread) in spreads.items():
        noise = np.random.default_rng([zlib.crc32(name.encode()), seed]).standard_normal(out[name].shape)
        drawn = base * np.exp(spread * noise) if base else spread * noise
        out[name] = jnp.asarray(drawn.astype(out[name].dtype))
    for name, factor in factors.items():
        out[name] = (out[name] * factor).astype(out[name].dtype)
    return out
```

```python
from contextlib import ExitStack
from concourse import mybir
import concourse.bass as bass

F32 = mybir.dt.float32
F16 = mybir.dt.float16
BF16 = mybir.dt.bfloat16
F8 = mybir.dt.float8e4
U32 = mybir.dt.uint32
I32 = mybir.dt.int32
ALU = mybir.AluOpType
ACT = mybir.ActivationFunctionType
X = mybir.AxisListType.X

P = 128
HEADS, OUT, ATT = 4, 16, 16
SLOTS = 4
BIG = 1.0e9
SKIP = 100000.0
SLOPE = 0.2
SCALE = 1.0 / ATT ** 0.5
EPS = 1.0e-5

STEPS_EXTRACT, STEPS_LIST, STEPS_LONG, STEPS_ATTEND, STEPS_AGG = 17, 2, 16, 16, 7
LONG_TEST = ALU.not_equal


def gat_resnorm_kernel(nc, x, adj, w_feat, w_self, w_other, bias, out):
    B, N, F = x.shape
    T = -(-N // P)
    ROWS = [min(P, N - P * t) for t in range(T)]
    LAST = ROWS[-1]
    LAST16 = LAST // 16 * 16
    HO = HEADS * OUT
    C = HO + 2 * F
    GROUPS = T // 3
    HALF = F * 3
    assert T % 4 == 0 and T % 3 == 0 and F == HO and B % 2 == 0

    ctx = ExitStack()

    def sb(name, shape, dt=F32):
        return ctx.enter_context(nc.sbuf_tensor(name, shape, dt))

    def ps(name, shape, dt=F32):
        return ctx.enter_context(nc.psum_tensor(name, shape, dt))

    def sem(name):
        return ctx.enter_context(nc.semaphore(name))

    with ctx:
        table = [nc.dram_tensor(f"table{p}", (N, 2 * F), F32, kind="Internal").ap() for p in range(2)]
        long_x1_dram = [nc.dram_tensor(f"long_x1_{p}", (T * P, F), F32, kind="Internal").ap() for p in range(2)]
        adj_rows = adj.rearrange("b n m -> (b n) m")
        x_rows = x.rearrange("b n f -> (b n) f")

        adj_in = sb("adj_in", [P, 4, N])
        x_in = [sb(f"x_in{p}", [P, T, F]) for p in range(2)]
        proj = [sb(f"proj{p}", [P, T, C]) for p in range(2)]
        otherT = [sb(f"otherT{p}", [P, N]) for p in range(2)]
        adjT = [sb(f"adjT{p}", [P, T, N], F8) for p in range(2)]
        keys = [sb(f"keys{p}", [P, T, 8]) for p in range(2)]
        valid = [sb(f"valid{p}", [P, T, SLOTS]) for p in range(2)]
        penalty = [sb(f"penalty{p}", [P, T, SLOTS]) for p in range(2)]
        degree = [sb(f"degree{p}", [P, T]) for p in range(2)]
        is_long = [sb(f"is_long{p}", [P, T]) for p in range(2)]
        index = [sb(f"index{p}", [P, T, SLOTS], U32) for p in range(2)]
        index_skip = sb("index_skip", [P, 3, SLOTS])
        gathered = [sb(f"gathered{p}", [P, T, SLOTS, 2 * F]) for p in range(2)]
        key_found = sb("key_found", [P, T])
        long16 = sb("long16", [P, T], F16)
        rank_sums = sb("rank_sums", [P, 2 * T])
        tile_end = sb("tile_end", [P, T])
        rank = [sb(f"rank{p}", [P, T]) for p in range(2)]
        tiles_over = sb("tiles_over", [P, T])
        tiles_used = sb("tiles_used", [P, 1])
        span = sb("span", [P, 2])
        span_int = [sb(f"span_int{p}", [P, 2], I32) for p in range(2)]
        list_vals = sb("list_vals", [P, 2])
        list_skip = sb("list_skip", [P, 1])
        first_row = sb("first_row", [P, 2])
        load_index = [sb(f"load_index{p}", [P, 1], U32) for p in range(2)]
        inv_degree = sb("inv_degree", [P, T])
        store_index = [sb(f"store_index{p}", [P, 1], U32) for p in range(2)]
        long_adj = sb("long_adj", [P, N])
        long_x = sb("long_x", [P, F])
        long_xT = sb("long_xT", [F, P])
        long_selfT = sb("long_selfT", [P, P])
        weights = [sb(f"weights{k}", [P, N]) for k in range(2)]
        xT = weights[0][0:F, :]
        row_max = sb("row_max", [P, HEADS])
        row_lrelu = sb("row_lrelu", [P, HEADS])
        neg_max = sb("neg_max", [P, HEADS])
        row_sum = sb("row_sum", [P, HEADS])
        row_rcp = sb("row_rcp", [P, HEADS])
        long_a = sb("long_a", [P, 1, F])
        long_b = sb("long_b", [P, 1, F])
        long_sq = sb("long_sq", [P, 1, F])
        long_stat = sb("long_stat", [P, 4])
        long_x1 = sb("long_x1", [P, F])
        prod = sb("prod", [P, T * SLOTS * F])
        onehot = prod[:, 0:T * P // 2].bitcast(F16).rearrange("p (t e) -> p t e", t=T)
        weightsT = prod[:, T * P:2 * T * P].rearrange("p (t e) -> p t e", t=T)
        score = sb("score", [P, T * SLOTS * HEADS])
        lrelu = sb("lrelu", [P, T * SLOTS * HEADS])
        slot_max = sb("slot_max", [P, T * HEADS])
        expw = sb("expw", [P, T * SLOTS * HEADS])
        den = sb("den", [P, T * HEADS])
        u = sb("u", [P, T, F])
        uc = sb("uc", [P, T, F])
        sq = sb("sq", [P, T, F])
        stat = sb("stat", [P, 4, T])
        x1 = sb("x1", [P, T, F])
        merged = sb("merged", [P, T, F])
        x1_parts = sb("x1_parts", [P, T, 3, F], BF16)
        y = uc
        ident = sb("ident", [P, P])
        w_all = sb("w_all", [F, C])
        w_self_pad = sb("w_self_pad", [F, P])
        w_other_pad = sb("w_other_pad", [F, P])
        bias_bc = sb("bias_bc", [P, HO])
        key_iota = sb("key_iota", [P, T])
        key_mat = sb("key_mat", [P, T, P + 1], F16)
        before = sb("before", [P, P], F16)
        ones = sb("ones", [P, P], F16)
        col_iota = sb("col_iota", [P, P])
        row_names = sb("row_names", [P, T, 2], F16)
        tile_steps = sb("tile_steps", [P, T])
        zero_row = sb("zero_row", [P, T])

        ring = ps("ring", [P, 4, 512])
        mid = ps("mid", [P, 3, 512])
        misc = ps("misc", [P, 512])
        rank_ps = misc[:, 0:2 * T]
        list_ps = misc[:, 32:34]
        long_out = misc[:, 64:64 + HO]
        long_xT_ps = misc[0:F, 128:256]
        long_selfT_ps = misc[:, 256:384]

        weights_in, const_ready, cleared, key_mat_ready, first_contents, psum_cleared = (
            sem("weights_in"), sem("const_ready"), sem("cleared"), sem("key_mat_ready"), sem("first_contents"),
            sem("psum_cleared"))
        scratch_init, pad_ready, mask_ready = sem("scratch_init"), sem("pad_ready"), sem("mask_ready")
        x_loaded = [sem(f"x_loaded{p}") for p in range(2)]
        xT_ps_ready, xT_ready = sem("xT_ps_ready"), sem("xT_ready")
        proj_ps_ready, proj_ready = sem("proj_ps_ready"), sem("proj_ready")
        otherT_ps_ready, otherT_ready = sem("otherT_ps_ready"), sem("otherT_ready")
        table_written = [sem(f"table_written{p}") for p in range(2)]
        adj_loaded = [sem(f"adj_loaded{s}") for s in range(4)]
        adj_transposed = sem("adj_transposed")
        adjT_by_act, adjT_by_dve = sem("adjT_by_act"), sem("adjT_by_dve")
        keys_ps_ready, keys_taken, index_ready = sem("keys_ps_ready"), sem("keys_taken"), sem("index_ready")
        extract_step, long16_ready, rank_ps_ready, span_ready = (
            sem("extract_step"), sem("long16_ready"), sem("rank_ps_ready"), sem("span_ready"))
        first_list = [sem(f"first_list_{s}") for s in ("onehot", "ps", "step", "ready")]
        more_list = [sem(f"more_list_{s}") for s in ("onehot", "ps", "step", "ready")]
        rank_moved = sem("rank_moved")
        slots_loaded = [sem(f"slots_loaded{p}") for p in range(2)]
        attend_step, exp_in_ready, exp_ready, gathered_read = (
            sem("attend_step"), sem("exp_in_ready"), sem("exp_ready"), sem("gathered_read"))
        centred, squared, var_ready, rstd_ready, ln_ready = (
            sem("centred"), sem("squared"), sem("var_ready"), sem("rstd_ready"), sem("ln_ready"))
        part_in_ready, part_ready, parts_ready = sem("part_in_ready"), sem("part_ready"), sem("parts_ready")
        long_loaded, long_xT_ps_ready, long_xT_ready = sem("long_loaded"), sem("long_xT_ps_ready"), sem("long_xT_ready")
        selfT_ps_ready, selfT_ready = sem("selfT_ps_ready"), sem("selfT_ready")
        long_step, scores_ready, scores_read, neg_max_ready = (
            sem("long_step"), sem("scores_ready"), sem("scores_read"), sem("neg_max_ready"))
        weights_ready, weights_transposed = sem("weights_ready"), sem("weights_transposed")
        weightsT_by_dve, weightsT_by_act, long_out_ready = (
            sem("weightsT_by_dve"), sem("weightsT_by_act"), sem("long_out_ready"))
        long_centred, long_squared, long_var, long_ln, long_rstd = (
            sem("long_centred"), sem("long_squared"), sem("long_var"), sem("long_ln"), sem("long_rstd"))
        long_x1_ready, long_stored = sem("long_x1_ready"), sem("long_stored")
        merged_loaded = [sem(f"merged_loaded{p}") for p in range(2)]
        agg_ps_ready, agg_read, agg_step, agg_done, y_ready, y_stored = (
            sem("agg_ps_ready"), sem("agg_read"), sem("agg_step"), sem("agg_done"), sem("y_ready"), sem("y_stored"))

        class Batch:

            def __init__(self, j, p, r):
                self.j, self.p, self.r = j, p, r

        AGG0, ATTEND0, LONG0, Y0, OTHER0 = T // 2 + 1, 2, 1, 1, 1
        RING0, RING_ACT0, RING_DVE0 = 12, 4, 2
        starts = ((agg_ps_ready, AGG0), (agg_read, AGG0), (gathered_read, ATTEND0), (parts_ready, ATTEND0),
                  (long_out_ready, LONG0), (scores_read, LONG0), (weightsT_by_act, LONG0), (weightsT_by_dve, LONG0),
                  (y_stored, Y0), (otherT_ps_ready, OTHER0), (adj_transposed, RING0), (adjT_by_act, RING_ACT0),
                  (adjT_by_dve, RING_DVE0))
        wait_passed = {e: sem(f"wait_passed_{e}") for e in ("Pool", "Activation", "PE", "DVE", "SP")}

        def alone(eng):
            eng.sem_inc(wait_passed[str(eng.engine).split(".")[-1]], 1)

        def chain(eng, semaphore, base):
            count = [0]

            def step(instruction):
                count[0] += 1
                instruction.then_inc(semaphore, 1)
                eng.wait_ge(semaphore, base + count[0])
            step.count = lambda: count[0]
            return step

        def pipeline(eng, extract, rest):
            extract(Batch(0, 0, 0))
            with eng.Fori(0, B // 2 - 1) as k:
                extract(Batch(2 * k + 1, 1, k))
                rest(Batch(2 * k, 0, k), 2 * k + 2)
                extract(Batch(2 * k + 2, 0, k + 1))
                rest(Batch(2 * k + 1, 1, k), 2 * k + 3)
            extract(Batch(B - 1, 1, B // 2 - 1))
            rest(Batch(B - 2, 0, B // 2 - 1), B)
            rest(Batch(B - 1, 1, B // 2 - 1), B)

        def load_span(eng, b):
            eng.wait_ge(span_ready, b.j + 1)
            alone(eng)
            first = eng.value_load(span_int[b.p][0:1, 0:1], min_val=0, max_val=B * T)
            end = eng.value_load(span_int[b.p][0:1, 1:2], min_val=1, max_val=B * T)
            return first, end

        def row_dmas(eng, dram, j, tile, store, semaphore):
            for rows, count, t0, t1 in ((0, P, 0, T - 1), (P * (T - 1), LAST16, T - 1, T),
                                        (P * (T - 1) + LAST16, LAST - LAST16, T - 1, T)):
                side = dram[bass.ds(j, 1), rows:rows + (t1 - t0) * count, :].rearrange(
                    "o (t p) f -> p (o t) f", p=count)
                at = rows % P
                part = tile[at:at + count, t0:t1, :]
                src, dst = (part, side) if store else (side, part)
                eng.dma_start(dst, src).then_inc(semaphore, 16)

        block = ctx.enter_context(nc.Block())

        @block.sync
        def _(sp):
            for dst, w in ((w_all[:, 0:F], w_self), (w_all[:, F:2 * F], w_other), (w_all[:, 2 * F:C], w_feat)):
                sp.dma_start(dst.rearrange("f (h o) -> f h o", h=HEADS),
                             w.rearrange("h f o -> f h o")).then_inc(weights_in, 16)
            sp.wait_ge(pad_ready, 3)
            for dst, w in ((w_self_pad, w_self), (w_other_pad, w_other)):
                sp.dma_start(dst[:, :].rearrange("f (h o) -> f h o", h=HEADS)[:, :, 0:ATT],
                             w.rearrange("h f o -> f h o")).then_inc(weights_in, 16)
            sp.dma_start(bias_bc[:, :], bias.rearrange("a b h o -> (a b) (h o)").broadcast_to([P, HO])
                         ).then_inc(weights_in, 16)

            def load_x(b):
                row_dmas(sp, x, b.j, x_in[b.p], False, x_loaded[b.p])

            def load_adj(b, tiles):
                for t in tiles:
                    s = t % 4
                    sp.wait_ge(adj_transposed, RING0 + 3 * (T * b.j + t - 3))
                    for r0, r1 in ((0, P),) if t < T - 1 else ((0, LAST16), (LAST16, LAST)):
                        sp.dma_start(adj_in[r0:r1, s, :], adj[bass.ds(b.j, 1), P * t + r0:P * t + r1, :].rearrange(
                            "o p m -> p (o m)")).then_inc(adj_loaded[s], 16)

            def load_rest(b):
                load_adj(b, range(4, 8))
                sp.wait_ge(proj_ready, (T // 2) * (b.j + 1))
                sp.wait_ge(parts_ready, ATTEND0 + b.j - 1)
                for r0, r1, t0, t1 in ((0, P, 0, T - 1), (0, LAST16, T - 1, T), (LAST16, LAST, T - 1, T)):
                    row0 = P * t0 + r0
                    rows = table[b.p][row0:row0 + (r1 - r0) * (t1 - t0), :].rearrange("(t p) f -> p t f", p=r1 - r0)
                    sp.dma_start(rows, proj[b.p][r0:r1, t0:t1, F:C]).then_inc(table_written[b.p], 16)
                load_adj(b, range(8, T))

            def read_back(b):
                first, end = load_span(sp, b)
                sp.wait_ge(long_stored, 16 * end)
                sp.wait_ge(parts_ready, ATTEND0 + b.j)
                sp.dma_start(merged[:, :, :], long_x1_dram[b.p].rearrange("(t p) f -> p t f", p=P)
                             ).then_inc(merged_loaded[b.p], 16)

            def store_y(b):
                sp.wait_ge(y_ready, b.j + 1)
                row_dmas(sp, out, b.j, y, True, y_stored)

            def step(b, next_b, after_next):
                if next_b:
                    load_rest(next_b)
                if after_next:
                    load_adj(after_next, range(4))
                read_back(b)
                if after_next:
                    sp.wait_ge(parts_ready, ATTEND0 + b.j + 1)
                    load_x(after_next)
                store_y(b)

            batch0, batch1 = Batch(0, 0, 0), Batch(1, 1, 0)
            load_x(batch0)
            load_x(batch1)
            load_adj(batch0, range(4))
            sp.wait_ge(cleared, 1)
            for p in range(2):
                sp.dma_start(long_x1_dram[p].rearrange("(p a) f -> p (a f)", p=P),
                             sq[:, :, :].rearrange("p t f -> p (t f)")).then_inc(scratch_init, 16)
            load_rest(batch0)
            load_adj(batch1, range(4))
            with sp.Fori(0, B // 2 - 1) as k:
                step(Batch(2 * k, 0, k), Batch(2 * k + 1, 1, k), Batch(2 * k + 2, 0, k + 1))
                step(Batch(2 * k + 1, 1, k), Batch(2 * k + 2, 0, k + 1), Batch(2 * k + 3, 1, k + 1))
            step(Batch(B - 2, 0, B // 2 - 1), Batch(B - 1, 1, B // 2 - 1), None)
            step(Batch(B - 1, 1, B // 2 - 1), None, None)
            sp.wait_ge(y_stored, Y0 + 48 * B)

        @block.gpsimd
        def _(pool):
            for semaphore, count in starts:
                pool.sem_inc(semaphore, count)
            pool.memset(w_self_pad[:, :], 0.0)
            pool.memset(w_other_pad[:, :], 0.0).then_inc(pad_ready, 1)
            for p in range(2):
                pool.memset(x_in[p][:, T - 1, :], 0.0).then_inc(pad_ready, 1)
            pool.memset(sq[:, :, :], 0.0).then_inc(cleared, 1)
            pool.memset(ident[:, :], 0.0).then_inc(mask_ready, 1)
            pool.memset(before[:, :], 1.0).then_inc(mask_ready, 1)
            pool.memset(ones[:, :], 1.0).then_inc(const_ready, 1)
            pool.memset(row_names[:, :, 1:2], 1.0).then_inc(const_ready, 1)
            pool.iota(key_iota[:, :], pattern=[[P, T]], base=1, channel_multiplier=1,
                      allow_small_or_imprecise_dtypes=True).then_inc(const_ready, 1)
            pool.iota(col_iota[:, :], pattern=[[1, P]], base=0, channel_multiplier=0,
                      allow_small_or_imprecise_dtypes=True).then_inc(const_ready, 1)
            pool.iota(row_names[:, :, 0:1], pattern=[[P, T]], base=0, channel_multiplier=1,
                      allow_small_or_imprecise_dtypes=True).then_inc(const_ready, 1)
            pool.iota(tile_steps[:, :], pattern=[[P, T]], base=0, channel_multiplier=0,
                      allow_small_or_imprecise_dtypes=True).then_inc(mask_ready, 1)
            pool.wait_ge(mask_ready, 3)
            pool.affine_select(out=ident[:, :], in_=ident[:, :], compare_op=ALU.not_equal, fill=1.0,
                               base=0, pattern=[[-1, P]], channel_multiplier=1).then_inc(const_ready, 1)
            pool.affine_select(out=before[:, :], in_=before[:, :], compare_op=ALU.is_gt, fill=0.0,
                               base=0, pattern=[[1, P]], channel_multiplier=-1).then_inc(const_ready, 1)
            pool.memset(tile_steps[:, 0:1], -1.0).then_inc(const_ready, 1)
            pool.memset(gathered[0][:, :, :, :], 0.0).then_inc(cleared, 1)
            pool.memset(gathered[1][:, :, :, :], 0.0).then_inc(cleared, 1)

            def gather_slots(b, groups):
                if groups[0] == 0:
                    pool.wait_ge(table_written[b.p], 48 * (b.r + 1))
                    pool.wait_ge(gathered_read, ATTEND0 + b.j - 1)
                for g in groups:
                    pool.wait_ge(index_ready, GROUPS * b.j + g + 1)
                    alone(pool)
                    for t in range(3 * g, 3 * g + 3):
                        for s in range(SLOTS):
                            pool.indirect_dma_start(
                                gathered[b.p][0:ROWS[t], t, s, :], None, table[b.p],
                                bass.IndirectOffsetOnAxis(ap=index[b.p][0:ROWS[t], t, s:s + 1], axis=0),
                                bounds_check=N - 1, oob_is_err=False).then_inc(slots_loaded[b.p], 16)

            def load_long(b, q):
                for dst, src in ((long_adj, adj_rows), (long_x, x_rows)):
                    pool.indirect_dma_start(dst[:, :], None, src,
                                            bass.IndirectOffsetOnAxis(ap=load_index[b.p][:, 0:1], axis=0),
                                            bounds_check=B * N - 1, oob_is_err=False).then_inc(long_loaded, 16)

            def store_long(b, q):
                pool.wait_ge(long_x1_ready, q + 1)
                alone(pool)
                pool.indirect_dma_start(long_x1_dram[b.p],
                                        bass.IndirectOffsetOnAxis(ap=store_index[b.p][:, 0:1], axis=0),
                                        long_x1[:, :], None,
                                        bounds_check=T * P - 1, oob_is_err=False).then_inc(long_stored, 16)

            def start_long(b):
                first, end = load_span(pool, b)
                pool.wait_ge(first_list[3], b.j + 1)
                alone(pool)
                load_long(b, first)

            def finish_long(b):
                first, end = load_span(pool, b)
                store_long(b, first)
                with pool.If(end - first > 1):
                    with pool.Fori(first + 1, end) as q:
                        pool.wait_ge(more_list[3], q + 1)
                        alone(pool)
                        load_long(b, q)
                        store_long(b, q)

            def next_batch(b, done):
                gather_slots(b, [0, 1])
                finish_long(done)
                start_long(b)
                gather_slots(b, [2, 3])

            batch0 = Batch(0, 0, 0)
            pool.wait_ge(scratch_init, 32)
            pool.wait_ge(cleared, 3)
            gather_slots(batch0, range(GROUPS))
            start_long(batch0)
            with pool.Fori(0, B // 2 - 1) as k:
                next_batch(Batch(2 * k + 1, 1, k), Batch(2 * k, 0, k))
                next_batch(Batch(2 * k + 2, 0, k + 1), Batch(2 * k + 1, 1, k))
            next_batch(Batch(B - 1, 1, B // 2 - 1), Batch(B - 2, 0, B // 2 - 1))
            finish_long(Batch(B - 1, 1, B // 2 - 1))

        @block.tensor
        def _(pe):
            pe.wait_ge(weights_in, 16 * 6)
            pe.wait_ge(const_ready, 8)
            pe.wait_ge(key_mat_ready, 1)
            pe.wait_ge(psum_cleared, 1)

            def project(b):
                pe.wait_ge(agg_read, AGG0 + (T // 2) * (b.j - 1))
                pe.wait_ge(x_loaded[b.p], 48 * (b.r + 1))
                alone(pe)
                for t in range(T):
                    last = pe.transpose(mid[0:F, t // 4, P * (t % 4):P * (t % 4) + ROWS[t]],
                                        x_in[b.p][0:ROWS[t], t, :], ident[0:ROWS[t], 0:ROWS[t]])
                    if t % 4 == 3:
                        last.then_inc(xT_ps_ready, 1)
                for g in range(T // 2):
                    if g < 3:
                        pe.wait_ge(xT_ready, 3 * b.j + g + 1)
                    else:
                        pe.wait_ge(proj_ready, (T // 2) * b.j + g - 2)
                    for t in (2 * g, 2 * g + 1):
                        pe.wait_ge(xT_ready, 3 * b.j + t // 4 + 1)
                        last = pe.matmul(mid[0:ROWS[t], g % 3, 256 * (t % 2):256 * (t % 2) + C],
                                         xT[:, P * t:P * t + ROWS[t]], w_all[:, :], start=True, stop=True)
                    last.then_inc(proj_ps_ready, 1)
                for c in range(3):
                    pe.wait_ge(proj_ready, (T // 2) * b.j + 3 + c + 1)
                    cols = min(512, N - 512 * c)
                    pe.matmul(mid[:, c, 0:cols], w_other_pad[:, :], xT[:, 512 * c:512 * c + cols],
                              start=True, stop=True).then_inc(otherT_ps_ready, 1)

            def transpose_tile(b, t):
                s = t % 4
                more = 16 if t == T - 1 else 0
                loads = 64 if s == 3 else 48
                pe.wait_ge(adj_loaded[s], loads * b.j + 16 * (t // 4 + 1) + more)
                for k in range(3):
                    v = 3 * t + k - 4
                    tt, kk = v // 3, v % 3
                    if kk == 2:
                        pe.wait_ge(adjT_by_dve, RING_DVE0 + T * b.j + tt + 1)
                    else:
                        pe.wait_ge(adjT_by_act, RING_ACT0 + 2 * T * b.j + 2 * tt + kk + 1)
                    for c in range(4 * k, 4 * k + 4):
                        last = pe.transpose(ring[0:ROWS[c], (3 * t + k) % 4, P * (c % 4):P * (c % 4) + ROWS[t]],
                                            adj_in[0:ROWS[t], s, P * c:P * c + ROWS[c]],
                                            ident[0:ROWS[t], 0:ROWS[t]])
                    last.then_inc(adj_transposed, 1)

            def keys_of_tile(b, t):
                g = t // 3
                if t % 3 == 0:
                    if g < 3:
                        pe.wait_ge(otherT_ready, 3 * b.j + g + 1)
                    else:
                        pe.wait_ge(keys_taken, GROUPS * b.j + g - 2)
                pe.wait_ge(adjT_by_act, RING_ACT0 + 2 * T * b.j + 2 * t + 2)
                pe.wait_ge(adjT_by_dve, RING_DVE0 + T * b.j + t + 1)
                alone(pe)
                for c in range(T):
                    last = pe.matmul(mid[0:ROWS[t], g % 3, (P + 1) * (t % 3):(P + 1) * (t % 3 + 1)],
                                     adjT[b.p][0:ROWS[c], c, P * t:P * t + ROWS[t]],
                                     key_mat[0:ROWS[c], c, :], start=(c == 0), stop=(c == T - 1))
                if t % 3 == 2:
                    last.then_inc(keys_ps_ready, 1)

            def list_rows(sems, count):
                pe.wait_ge(sems[0], count)
                for t in range(T):
                    last = pe.matmul(list_ps, onehot[:, t, :], row_names[:, t, :],
                                     start=(t == 0), stop=(t == T - 1))
                last.then_inc(sems[1], 1)

            def extract(b):
                project(b)
                for t in range(T):
                    transpose_tile(b, t)
                    if t > 0:
                        keys_of_tile(b, t - 1)
                keys_of_tile(b, T - 1)
                pe.wait_ge(long16_ready, b.j + 1)
                pe.matmul(rank_ps[:, 0:T], before[:, :], long16[:, :], start=True, stop=True)
                pe.matmul(rank_ps[:, T:2 * T], ones[:, :], long16[:, :], start=True, stop=True
                          ).then_inc(rank_ps_ready, 1)
                list_rows(first_list, b.j + 1)

            def long_scores(b, q, h):
                pe.wait_ge(scores_read, LONG0 + HEADS * q + h)
                for c in range(3):
                    cols = min(512, N - 512 * c)
                    last = pe.matmul(mid[:, c, 0:cols], long_selfT[32 * h:32 * h + ATT, :],
                                     otherT[b.p][32 * h:32 * h + ATT, 512 * c:512 * c + cols],
                                     start=True, stop=True)
                last.then_inc(scores_ready, 1)

            def long_transposes(q, h):
                pe.wait_ge(weights_ready, HEADS * q + h + 1)
                for k in range(3):
                    if k < 2:
                        pe.wait_ge(weightsT_by_dve, LONG0 + 2 * (HEADS * q + h))
                    else:
                        pe.wait_ge(weightsT_by_act, LONG0 + HEADS * q + h)
                    for c in range(4 * k, 4 * k + 4):
                        last = pe.transpose(ring[0:ROWS[c], k, P * (c % 4):P * (c % 4) + P],
                                            weights[h % 2][:, P * c:P * c + ROWS[c]], ident[:, :])
                    last.then_inc(weights_transposed, 1)

            def long_products(b, q, h):
                pe.wait_ge(weightsT_by_dve, LONG0 + 2 * (HEADS * q + h + 1))
                pe.wait_ge(weightsT_by_act, LONG0 + HEADS * q + h + 1)
                for c in range(T):
                    last = pe.matmul(long_out[:, OUT * h:OUT * (h + 1)], weightsT[0:ROWS[c], c, :],
                                     proj[b.p][0:ROWS[c], c, 2 * F + OUT * h:2 * F + OUT * (h + 1)],
                                     start=(c == 0), stop=(c == T - 1))
                last.then_inc(long_out_ready, 1)

            def long_tile(b, q):
                pe.wait_ge(long_loaded, 32 * (q + 1))
                alone(pe)
                pe.transpose(long_xT_ps, long_x[:, :], ident[:, :]).then_inc(long_xT_ps_ready, 1)
                pe.wait_ge(long_xT_ready, q + 1)
                pe.matmul(long_selfT_ps, w_self_pad[:, :], long_xT[:, :], start=True, stop=True
                          ).then_inc(selfT_ps_ready, 1)
                pe.wait_ge(selfT_ready, q + 1)
                long_scores(b, q, 0)
                for h in range(HEADS):
                    if h + 1 < HEADS:
                        long_scores(b, q, h + 1)
                    long_transposes(q, h)
                    long_products(b, q, h)

            def rest(b, extracted):
                pe.wait_ge(adjT_by_act, RING_ACT0 + 2 * T * extracted)
                pe.wait_ge(adjT_by_dve, RING_DVE0 + T * extracted)
                pe.wait_ge(keys_taken, GROUPS * extracted)
                pe.wait_ge(first_list[3], extracted)
                first, end = load_span(pe, b)
                pe.sem_inc(more_list[1], 1)
                long_tile(b, first)
                with pe.If(end - first > 1):
                    with pe.Fori(first + 1, end) as q:
                        list_rows(more_list, q + 1)
                        pe.wait_ge(more_list[3], q + 1)
                        long_tile(b, q)
                pe.wait_ge(weightsT_by_dve, LONG0 + 2 * HEADS * end)
                pe.wait_ge(weightsT_by_act, LONG0 + HEADS * end)
                pe.wait_ge(scores_read, LONG0 + HEADS * end)
                pe.wait_ge(parts_ready, ATTEND0 + b.j + 1)
                for t in range(T):
                    g = t // 2
                    if t % 2 == 0 and g >= 3:
                        pe.wait_ge(agg_read, AGG0 + (T // 2) * b.j + g - 2)
                    if t % 2 == 0 and (g == 0 or g >= 3):
                        alone(pe)
                    for c in range(T):
                        last = pe.matmul(mid[0:ROWS[t], g % 3, 256 * (t % 2):256 * (t % 2) + 3 * F],
                                         adjT[b.p][0:ROWS[c], c, P * t:P * t + ROWS[t]],
                                         x1_parts[0:ROWS[c], c, :, :].rearrange("p a f -> p (a f)"),
                                         start=(c == 0), stop=(c == T - 1))
                    if t % 2 == 1:
                        last.then_inc(agg_ps_ready, 1)

            pipeline(pe, extract, rest)

        @block.scalar
        def _(act):
            act.wait_ge(scratch_init, 32)

            def extract(b):
                for u3 in range(3):
                    act.wait_ge(xT_ps_ready, 3 * b.j + u3 + 1)
                    if u3 == 0:
                        act.wait_ge(otherT_ps_ready, OTHER0 + 3 * b.j)
                    cols = min(512, N - 512 * u3)
                    act.copy(xT[:, 512 * u3:512 * u3 + cols], mid[0:F, u3, 0:cols]).then_inc(xT_ready, 1)
                act.wait_ge(parts_ready, ATTEND0 + b.j - 1)
                for g in range(T // 2):
                    act.wait_ge(proj_ps_ready, (T // 2) * b.j + g + 1)
                    act.copy(proj[b.p][:, 2 * g:2 * g + 2, :],
                             mid[:, g % 3, :].rearrange("p (t c) -> p t c", t=2)[:, :, 0:C]
                             ).then_inc(proj_ready, 1)
                for c in range(3):
                    act.wait_ge(otherT_ps_ready, OTHER0 + 3 * b.j + c + 1)
                    cols = min(512, N - 512 * c)
                    act.copy(otherT[b.p][:, 512 * c:512 * c + cols], mid[:, c, 0:cols]).then_inc(otherT_ready, 1)
                act.wait_ge(agg_ps_ready, AGG0 + (T // 2) * (b.j - 1))
                for t in range(T):
                    for k in range(2):
                        act.wait_ge(adj_transposed, RING0 + 3 * (T * b.j + t) + k + 1)
                        alone(act)
                        act.copy(adjT[b.p][:, 4 * k:4 * k + 4, P * t:P * t + ROWS[t]],
                                 ring[:, (3 * t + k) % 4, :].rearrange("p (c n) -> p c n", c=4)[:, :, 0:ROWS[t]],
                                 saturate=False).then_inc(adjT_by_act, 1)

            def long_tile(b, q):
                act.wait_ge(long_xT_ps_ready, q + 1)
                act.copy(long_xT[:, :], long_xT_ps).then_inc(long_xT_ready, 1)
                act.wait_ge(selfT_ps_ready, q + 1)
                act.copy(long_selfT[:, :], long_selfT_ps).then_inc(selfT_ready, 1)
                for h in range(HEADS):
                    n = HEADS * q + h
                    act.wait_ge(neg_max_ready, n + 1)
                    act.activation(weights[h % 2][:, :], weights[h % 2][:, :], ACT.Exp,
                                   bias=neg_max[:, h:h + 1], scale=SCALE,
                                   accum_out=row_sum[:, h:h + 1]).then_inc(weights_ready, 1)
                    act.wait_ge(weights_transposed, 3 * n + 3)
                    act.wait_ge(long_out_ready, LONG0 + n)
                    act.copy(weightsT[:, 8:12, :], ring[:, 2, :].rearrange("p (c n) -> p c n", c=4)
                             ).then_inc(weightsT_by_act, 1)
                act.wait_ge(long_centred, q + 1)
                act.activation(long_sq[:, :, :], long_b[:, :, :], ACT.Square).then_inc(long_squared, 1)
                act.wait_ge(long_var, q + 1)
                act.activation(long_stat[:, 2:3], long_stat[:, 1:2], ACT.Ln).then_inc(long_ln, 1)
                act.wait_ge(long_ln, q + 1)
                act.activation(long_stat[:, 3:4], long_stat[:, 2:3], ACT.Exp, scale=-0.5).then_inc(long_rstd, 1)

            def layernorm(n):
                act.wait_ge(centred, n)
                act.activation(sq[:, :, :], uc[:, :, :], ACT.Square).then_inc(squared, 1)
                act.wait_ge(var_ready, n)
                act.activation(stat[:, 2, :], stat[:, 1, :], ACT.Ln).then_inc(ln_ready, 1)
                act.wait_ge(ln_ready, n)
                act.activation(stat[:, 3, :], stat[:, 2, :], ACT.Exp, scale=-0.5).then_inc(rstd_ready, 1)

            def rest(b, extracted):
                first, end = load_span(act, b)
                with act.Fori(first, end) as q:
                    long_tile(b, q)
                act.wait_ge(exp_in_ready, b.j + 1)
                act.activation(expw[:, :], score[:, :], ACT.Exp, scale=SCALE).then_inc(exp_ready, 1)
                layernorm(2 * b.j + 1)
                act.wait_ge(part_in_ready, 2 * b.j + 1)
                act.wait_ge(agg_ps_ready, AGG0 + (T // 2) * b.j)
                act.copy(x1_parts[:, :, 0, :], x1[:, :, :]).then_inc(part_ready, 1)
                act.wait_ge(part_in_ready, 2 * b.j + 2)
                act.copy(x1_parts[:, :, 1, :], u[:, :, :]).then_inc(part_ready, 1)
                layernorm(2 * b.j + 2)

            pipeline(act, extract, rest)

        @block.vector
        def _(dve):
            dve.memset(ring[:, :, :], 0.0)
            dve.memset(mid[:, :, :], 0.0)
            dve.memset(misc[:, :], 0.0).then_inc(psum_cleared, 1)
            for p in range(2):
                dve.memset(keys[p][:, :, :], 0.0)
                dve.memset(degree[p][:, :], 0.0)
                dve.memset(first_row[:, p:p + 1], float(N * (p - 2)))
            dve.memset(zero_row[:, :], 0.0)
            dve.memset(span[:, :], 0.0)
            dve.memset(key_mat[:, :, P:P + 1], 1.0).then_inc(first_contents, 1)
            dve.wait_ge(first_contents, 1)
            dve.wait_ge(const_ready, 8)
            dve.tensor_tensor(key_mat[:, :, 0:P], ident[:, :].unsqueeze(1).broadcast_to([P, T, P]),
                              key_iota[:, :].unsqueeze(2).broadcast_to([P, T, P]), ALU.mult
                              ).then_inc(key_mat_ready, 1)
            dve.wait_ge(key_mat_ready, 1)
            dve.wait_ge(weights_in, 16 * 6)

            def make_list(b, sems, count):
                one_sem, ps_sem, step_sem, ready_sem = sems
                step = chain(dve, step_sem, STEPS_LIST * (count - 1))
                dve.tensor_tensor(onehot[:, :, :], rank[b.p][:, :].unsqueeze(2).broadcast_to([P, T, P]),
                                  col_iota[:, :].unsqueeze(1).broadcast_to([P, T, P]), ALU.is_equal
                                  ).then_inc(one_sem, 1)
                dve.wait_ge(ps_sem, count)
                step(dve.tensor_copy(list_vals[:, :], list_ps))
                dve.tensor_scalar(load_index[b.p][:, :], list_vals[:, 0:1], first_row[:, b.p:b.p + 1], None, ALU.add)
                step(dve.tensor_scalar(list_skip[:, :], list_vals[:, 1:2], -SKIP, SKIP, ALU.mult, ALU.add))
                dve.tensor_tensor(store_index[b.p][:, :], list_vals[:, 0:1], list_skip[:, :], ALU.add
                                  ).then_inc(ready_sem, 1)
                assert step.count() == STEPS_LIST

            def take_keys(b, g, step):
                dve.wait_ge(keys_ps_ready, GROUPS * b.j + g + 1)
                alone(dve)
                for t in range(3 * g, 3 * g + 3):
                    at = (P + 1) * (t % 3)
                    dve.max(keys[b.p][0:ROWS[t], t, :], mid[0:ROWS[t], g % 3, at:at + P])
                    last = dve.tensor_copy(degree[b.p][0:ROWS[t], t:t + 1], mid[0:ROWS[t], g % 3, at + P:at + P + 1])
                last.then_inc(keys_taken, 1)
                dve.wait_ge(keys_taken, GROUPS * b.j + g + 1)
                found = keys[b.p][:, 3 * g:3 * g + 3, 0:SLOTS]
                step(dve.tensor_scalar(index_skip[:, :, :], found, 0.5, SKIP, ALU.is_lt, ALU.mult))
                dve.scalar_tensor_tensor(index[b.p][:, 3 * g:3 * g + 3, :], found, -1.0, index_skip[:, :, :],
                                         ALU.add, ALU.add).then_inc(index_ready, 1)

            def extract(b):
                step = chain(dve, extract_step, STEPS_EXTRACT * b.j)
                step(dve.tensor_scalar(first_row[:, b.p:b.p + 1], first_row[:, b.p:b.p + 1], 2.0 * N, None, ALU.add))
                dve.wait_ge(agg_ps_ready, AGG0 + (T // 2) * (b.j - 1))
                for t in range(T):
                    dve.wait_ge(adj_transposed, RING0 + 3 * (T * b.j + t) + 3)
                    alone(dve)
                    chunk = ring[:, (3 * t + 2) % 4, :].rearrange("p (c n) -> p c n", c=4)
                    dve.tensor_copy(adjT[b.p][:, 8:12, P * t:P * t + ROWS[t]], chunk[:, :, 0:ROWS[t]],
                                    saturate=False).then_inc(adjT_by_dve, 1)
                    if t % 3 == 1 and t > 3:
                        take_keys(b, t // 3 - 1, step)
                take_keys(b, GROUPS - 1, step)

                step(dve.tensor_scalar(valid[b.p][:, :, :], keys[b.p][:, :, 0:SLOTS], 0.5, None, ALU.is_gt))
                dve.tensor_scalar(penalty[b.p][:, :, :], valid[b.p][:, :, :], 1.0, BIG, ALU.subtract, ALU.mult)
                step(dve.tensor_reduce(key_found[:, :], valid[b.p][:, :, :], X, ALU.add))
                step(dve.tensor_tensor(is_long[b.p][:, :], key_found[:, :], degree[b.p][:, :], LONG_TEST))
                dve.tensor_copy(long16[:, :], is_long[b.p][:, :]).then_inc(long16_ready, 1)
                dve.wait_ge(rank_ps_ready, b.j + 1)
                step(dve.tensor_copy(rank_sums[:, :], rank_ps))
                step(dve.tensor_tensor_scan(tile_end[:, :], rank_sums[:, T:2 * T], zero_row[:, :], 0.0,
                                            ALU.add, ALU.add))
                r = rank[b.p]
                step(dve.scalar_tensor_tensor(r[:, :], is_long[b.p][:, :], -1.0e4, rank_sums[:, 0:T], ALU.mult, ALU.add))
                step(dve.scalar_tensor_tensor(r[:, :], r[:, :], 1.0e4, tile_end[:, :], ALU.add, ALU.add))
                step(dve.tensor_tensor(r[:, :], r[:, :], rank_sums[:, T:2 * T], ALU.subtract))
                step(dve.tensor_scalar(tiles_over[:, :], tile_steps[:, :], tile_end[:, T - 1:T], None, ALU.is_lt))
                step(dve.tensor_reduce(tiles_used[:, :], tiles_over[:, :], X, ALU.add))
                step(dve.tensor_copy(span[:, 0:1], span[:, 1:2]))
                step(dve.tensor_tensor(span[:, 1:2], span[:, 1:2], tiles_used[:, :], ALU.add))
                dve.tensor_copy(span_int[b.p][:, :], span[:, :]).then_inc(span_ready, 1)
                make_list(b, first_list, b.j + 1)
                assert step.count() == STEPS_EXTRACT

            def long_max(step, q, h):
                n = HEADS * q + h
                dve.wait_ge(scores_ready, n + 1)
                if h >= 2:
                    dve.wait_ge(weights_transposed, 3 * (n - 1))
                alone(dve)
                dve.tensor_tensor_reduce(out=weights[h % 2][:, :],
                                         in0=mid[:, :, :].rearrange("p b n -> p (b n)")[:, 0:N], in1=long_adj[:, :],
                                         scale=1.0, scalar=-3.0e38, op0=ALU.add, op1=ALU.max,
                                         accum_out=row_max[:, h:h + 1]).then_inc(scores_read, 1)
                dve.wait_ge(scores_read, LONG0 + n + 1)
                step(dve.scalar_tensor_tensor(weights[h % 2][:, :], weights[h % 2][:, :], SLOPE, weights[h % 2][:, :],
                                              ALU.mult, ALU.max))
                step(dve.scalar_tensor_tensor(row_lrelu[:, h:h + 1], row_max[:, h:h + 1], SLOPE,
                                              row_max[:, h:h + 1], ALU.mult, ALU.max))
                dve.tensor_scalar(neg_max[:, h:h + 1], row_lrelu[:, h:h + 1], -SCALE, None, ALU.mult
                                  ).then_inc(neg_max_ready, 1)

            def long_copy(q, h):
                n = HEADS * q + h
                for k in range(2):
                    dve.wait_ge(weights_transposed, 3 * n + k + 1)
                    dve.wait_ge(long_out_ready, LONG0 + n)
                    dve.tensor_copy(weightsT[:, 4 * k:4 * k + 4, :],
                                    ring[:, k, :].rearrange("p (c n) -> p c n", c=4)).then_inc(weightsT_by_dve, 1)

            def long_tile(b, q):
                step = chain(dve, long_step, STEPS_LONG * q)
                dve.wait_ge(long_loaded, 32 * (q + 1))
                step(dve.tensor_scalar(long_adj[:, :], long_adj[:, :], 1.0, BIG, ALU.subtract, ALU.mult))
                long_max(step, q, 0)
                for h in range(HEADS):
                    if h + 1 < HEADS:
                        long_max(step, q, h + 1)
                    long_copy(q, h)
                dve.wait_ge(long_out_ready, LONG0 + HEADS * (q + 1))
                step(dve.reciprocal(row_rcp[:, :], row_sum[:, :]))
                la = long_a[:, 0, :]
                step(dve.tensor_tensor(la.rearrange("p (h o) -> p h o", h=HEADS),
                                       long_out.rearrange("p (h o) -> p h o", h=HEADS),
                                       row_rcp[:, :].unsqueeze(2).broadcast_to([P, HEADS, OUT]), ALU.mult))
                step(dve.tensor_tensor(la, la, bias_bc[:, :], ALU.add))
                step(dve.scalar_tensor_tensor(la, la, 0.0, long_x[:, :], ALU.max, ALU.add))
                step(dve.tensor_reduce(long_stat[:, 0:1], la, X, ALU.add))
                step(dve.tensor_scalar(long_stat[:, 0:1], long_stat[:, 0:1], 1.0 / F, None, ALU.mult))
                dve.tensor_scalar(long_b[:, 0, :], la, long_stat[:, 0:1], None, ALU.subtract).then_inc(long_centred, 1)
                dve.wait_ge(long_squared, q + 1)
                step(dve.tensor_reduce(long_stat[:, 1:2], long_sq[:, 0, :], X, ALU.add))
                dve.tensor_scalar(long_stat[:, 1:2], long_stat[:, 1:2], 1.0 / F, EPS, ALU.mult, ALU.add
                                  ).then_inc(long_var, 1)
                dve.wait_ge(long_rstd, q + 1)
                dve.tensor_scalar(long_x1[:, :], long_b[:, 0, :], long_stat[:, 3:4], None, ALU.mult
                                  ).then_inc(long_x1_ready, 1)
                assert step.count() == STEPS_LONG

            def over_features(v):
                return v.unsqueeze(2).broadcast_to([P, T, F])

            def layernorm(step, n, dst):
                step(dve.tensor_reduce(stat[:, 0, :], u[:, :, :], X, ALU.add))
                step(dve.tensor_scalar(stat[:, 0, :], stat[:, 0, :], 1.0 / F, None, ALU.mult))
                dve.tensor_tensor(uc[:, :, :], u[:, :, :], over_features(stat[:, 0, :]), ALU.subtract
                                  ).then_inc(centred, 1)
                dve.wait_ge(squared, n)
                step(dve.tensor_reduce(stat[:, 1, :], sq[:, :, :], X, ALU.add))
                dve.tensor_scalar(stat[:, 1, :], stat[:, 1, :], 1.0 / F, EPS, ALU.mult, ALU.add).then_inc(var_ready, 1)
                dve.wait_ge(rstd_ready, n)
                return dve.tensor_tensor(dst[:, :, :], uc[:, :, :], over_features(stat[:, 3, :]), ALU.mult)

            def attend(b):
                step = chain(dve, attend_step, STEPS_ATTEND * b.j)
                TS = T * SLOTS
                dve.wait_ge(y_stored, Y0 + 48 * b.j)
                dve.wait_ge(proj_ready, (T // 2) * (b.j + 1))
                dve.wait_ge(slots_loaded[b.p], 16 * TS * (b.r + 1))
                G = gathered[b.p]
                by_head = prod[:, :].rearrange("p (a h o) -> p a h o", h=HEADS, o=OUT)
                by_slot = "p (t s h) -> p t h s"
                step(dve.tensor_tensor(prod[:, :].rearrange("p (t s f) -> p t s f", t=T, s=SLOTS), G[:, :, :, 0:F],
                                       proj[b.p][:, :, 0:F].unsqueeze(2).broadcast_to([P, T, SLOTS, F]), ALU.mult))
                step(dve.tensor_reduce(score[:, :], prod[:, :].rearrange("p (a d) -> p a d", d=ATT), X, ALU.add))
                slot_head = score[:, :].rearrange("p (a h) -> p a h", h=HEADS)
                per_slot = penalty[b.p][:, :, :].rearrange("p t s -> p (t s)").unsqueeze(2).broadcast_to([P, TS, HEADS])
                step(dve.tensor_tensor(slot_head, slot_head, per_slot, ALU.add))
                step(dve.scalar_tensor_tensor(lrelu[:, :], score[:, :], SLOPE, score[:, :], ALU.mult, ALU.max))
                step(dve.tensor_reduce(slot_max[:, :].rearrange("p (t h) -> p t h", t=T),
                                       lrelu[:, :].rearrange(by_slot, t=T, s=SLOTS), X, ALU.max))
                dve.tensor_tensor(score[:, :].rearrange("p (t s h) -> p t s h", t=T, s=SLOTS),
                                  lrelu[:, :].rearrange("p (t s h) -> p t s h", t=T, s=SLOTS),
                                  slot_max[:, :].rearrange("p (t h) -> p t h", t=T).unsqueeze(2).broadcast_to(
                                      [P, T, SLOTS, HEADS]), ALU.subtract).then_inc(exp_in_ready, 1)
                dve.wait_ge(exp_ready, b.j + 1)
                step(dve.tensor_reduce(den[:, :].rearrange("p (t h) -> p t h", t=T),
                                       expw[:, :].rearrange(by_slot, t=T, s=SLOTS), X, ALU.add))
                slot_head = expw[:, :].rearrange("p (a h) -> p a h", h=HEADS)
                per_slot = valid[b.p][:, :, :].rearrange("p t s -> p (t s)").unsqueeze(2).broadcast_to([P, TS, HEADS])
                step(dve.tensor_tensor(slot_head, slot_head, per_slot, ALU.mult))
                dve.tensor_tensor(by_head, G[:, :, :, F:2 * F].rearrange("p t s (h o) -> p (t s) h o", h=HEADS),
                                  slot_head.unsqueeze(3).broadcast_to([P, TS, HEADS, OUT]), ALU.mult
                                  ).then_inc(gathered_read, 1)
                dve.wait_ge(gathered_read, ATTEND0 + b.j + 1)
                step(dve.tensor_reduce(u[:, :, :], prod[:, :].rearrange("p (t s f) -> p t f s", t=T, s=SLOTS), X, ALU.add))
                step(dve.reciprocal(den[:, :], den[:, :]))
                flat = u[:, :, :].rearrange("p t (h o) -> p (t h) o", h=HEADS)
                step(dve.tensor_tensor(flat, flat, den[:, :].unsqueeze(2).broadcast_to([P, T * HEADS, OUT]), ALU.mult))
                step(dve.tensor_tensor(u[:, :, :], u[:, :, :], bias_bc[:, :].unsqueeze(1).broadcast_to([P, T, HO]), ALU.add))
                step(dve.scalar_tensor_tensor(u[:, :, :], u[:, :, :], 0.0, x_in[b.p][:, :, :], ALU.max, ALU.add))
                step(layernorm(step, 2 * b.j + 1, x1))
                dve.wait_ge(merged_loaded[b.p], 16 * (b.r + 1))
                alone(dve)
                dve.copy_predicated(x1[:, :, :], over_features(is_long[b.p][:, :].bitcast(U32)), merged[:, :, :]
                                    ).then_inc(part_in_ready, 1)
                dve.wait_ge(part_ready, 2 * b.j + 1)
                dve.tensor_tensor(u[:, :, :], x1[:, :, :], x1_parts[:, :, 0, :], ALU.subtract).then_inc(part_in_ready, 1)
                dve.wait_ge(part_ready, 2 * b.j + 2)
                dve.tensor_tensor(x1_parts[:, :, 2, :], u[:, :, :], x1_parts[:, :, 1, :], ALU.subtract
                                  ).then_inc(parts_ready, 1)
                assert step.count() == STEPS_ATTEND

            def aggregate(b):
                step = chain(dve, agg_step, STEPS_AGG * b.j)
                messages = prod[:, 0:T * F].rearrange("p (t f) -> p t f", t=T)
                step(dve.tensor_scalar(inv_degree[:, :], degree[b.p][:, :], 1.0, None, ALU.max))
                step(dve.reciprocal(inv_degree[:, :], inv_degree[:, :]))
                for g in range(T // 2):
                    dve.wait_ge(agg_ps_ready, AGG0 + (T // 2) * b.j + g + 1)
                    parts = mid[:, g % 3, :].rearrange("p (t c) -> p t c", t=2)[:, :, 0:3 * F]
                    dve.tensor_reduce(messages[:, 2 * g:2 * g + 2, :], parts.rearrange("p t (a f) -> p t f a", a=3),
                                      X, ALU.add).then_inc(agg_read, 1)
                dve.wait_ge(agg_read, AGG0 + (T // 2) * (b.j + 1))
                step(dve.tensor_tensor(messages, messages, over_features(inv_degree[:, :]), ALU.mult))
                step(dve.tensor_tensor(u[:, :, :], messages, x1[:, :, :], ALU.add))
                layernorm(step, 2 * b.j + 2, y).then_inc(y_ready, 1)
                assert step.count() == STEPS_AGG

            def rest(b, extracted):
                first, end = load_span(dve, b)
                dve.sem_inc(more_list[0], 1)
                dve.sem_inc(more_list[2], STEPS_LIST)
                dve.sem_inc(more_list[3], 1)
                dve.sem_inc(rank_moved, 1)
                long_tile(b, first)
                with dve.If(end - first > 1):
                    with dve.Fori(first + 1, end) as q:
                        dve.wait_ge(long_stored, 16 * q)
                        step = chain(dve, rank_moved, q)
                        step(dve.tensor_scalar(rank[b.p][:, :], rank[b.p][:, :], float(P), None, ALU.subtract))
                        make_list(b, more_list, q + 1)
                        long_tile(b, q)
                attend(b)
                aggregate(b)

            pipeline(dve, extract, rest)


_INS = ['x', 'adj', 'L0_gnn_kernel', 'L0_gnn_attention_kernel', 'L0_gnn_attention_kernel_2', 'L0_gnn_bias']


def kernel(**inputs):
    import numpy as _np
    import concourse.bacc as _bacc
    from concourse import mybir as _mybir
    from concourse.bass_utils import run_bass_kernel_spmd as _run

    nc = _bacc.Bacc("TRN2", target_bir_lowering=False, num_devices=1)
    arrays, args = {}, []
    for name in _INS:
        a = _np.ascontiguousarray(inputs[name])
        arrays[f"in_{name}_dram"] = a
        args.append(nc.dram_tensor(f"in_{name}_dram", a.shape, _mybir.dt.from_np(a.dtype), kind="ExternalInput").ap())
    args.append(nc.dram_tensor("out_0_dram", inputs["x"].shape, _mybir.dt.float32, kind="ExternalOutput").ap())
    gat_resnorm_kernel(nc, *args)
    r = _run(nc, [arrays], core_ids=[0])
    return r.results[0]["out_0_dram"]
```

```python
from contextlib import ExitStack
from concourse import mybir
import concourse.bass as bass

F32 = mybir.dt.float32
F16 = mybir.dt.float16
BF16 = mybir.dt.bfloat16
F8 = mybir.dt.float8e4
U32 = mybir.dt.uint32
I32 = mybir.dt.int32
ALU = mybir.AluOpType
ACT = mybir.ActivationFunctionType
X = mybir.AxisListType.X

P = 128
HEADS, OUT, ATT = 4, 16, 16
SLOTS = 4
MSLOTS = 12
BIG = 1.0e9
SKIP = 100000.0
SLOPE = 0.2
SCALE = 1.0 / ATT ** 0.5
EPS = 1.0e-5

STEPS_EXTRACT, STEPS_LIST, STEPS_MEDIUM, STEPS_RANK, STEPS_LONG, STEPS_ATTEND, STEPS_AGG = 23, 2, 6, 7, 16, 16, 7
LONG_TEST = ALU.not_equal
MEDIUM_DEGREE = MSLOTS


def gat_resnorm_kernel(nc, x, adj, w_feat, w_self, w_other, bias, out):
    B, N, F = x.shape
    T = -(-N // P)
    ROWS = [min(P, N - P * t) for t in range(T)]
    LAST = ROWS[-1]
    LAST16 = LAST // 16 * 16
    HO = HEADS * OUT
    C = HO + 2 * F
    GROUPS = T // 3
    TS = T * SLOTS
    AS = TS + MSLOTS
    assert T % 4 == 0 and T % 3 == 0 and F == HO and B % 2 == 0

    ctx = ExitStack()

    def sb(name, shape, dt=F32):
        return ctx.enter_context(nc.sbuf_tensor(name, shape, dt))

    def ps(name, shape, dt=F32):
        return ctx.enter_context(nc.psum_tensor(name, shape, dt))

    def sem(name):
        return ctx.enter_context(nc.semaphore(name))

    with ctx:
        table = [nc.dram_tensor(f"table{p}", (N, 2 * F), F32, kind="Internal").ap() for p in range(2)]
        self_table = [nc.dram_tensor(f"self_table{p}", (N, F), F32, kind="Internal").ap() for p in range(2)]
        long_x1_dram = [nc.dram_tensor(f"long_x1_{p}", (T * P, F), F32, kind="Internal").ap() for p in range(2)]
        adj_rows = adj.rearrange("b n m -> (b n) m")
        x_rows = x.rearrange("b n f -> (b n) f")

        adj_in = sb("adj_in", [P, 4, N])
        x_in = [sb(f"x_in{p}", [P, T + 1, F]) for p in range(2)]
        proj = [sb(f"proj{p}", [P, T + 1, C]) for p in range(2)]
        adjT = [sb(f"adjT{p}", [P, T, N], F8) for p in range(2)]
        keys = sb("keys", [P, T, 8])
        valid = [sb(f"valid{p}", [P, AS]) for p in range(2)]
        penalty = [sb(f"penalty{p}", [P, AS]) for p in range(2)]
        degree = [sb(f"degree{p}", [P, T]) for p in range(2)]
        is_long = [sb(f"is_long{p}", [P, T]) for p in range(2)]
        index = [sb(f"index{p}", [P, T, SLOTS], U32) for p in range(2)]
        index_skip = sb("index_skip", [P, 3, SLOTS])
        gathered = [sb(f"gathered{p}", [P, T, SLOTS, 2 * F]) for p in range(2)]
        medium_gathered = sb("medium_gathered", [P, MSLOTS, 2 * F])
        medium_keys = sb("medium_keys", [P, 16])
        medium_skip = sb("medium_skip", [P, MSLOTS])
        medium_index = sb("medium_index", [P, MSLOTS], U32)
        node_iota = sb("node_iota", [P, N], F16)
        key_found = sb("key_found", [P, T])
        is_medium = sb("is_medium", [P, T])
        is_dense = sb("is_dense", [P, T])
        total_long = sb("total_long", [P, 1])
        long16 = sb("long16", [P, 2 * T], F16)
        dense16 = sb("dense16", [P, T], F16)
        rank_sums = sb("rank_sums", [P, 3 * T])
        tile_end = sb("tile_end", [P, T])
        rank = [sb(f"rank{p}", [P, T]) for p in range(2)]
        tiles_over = sb("tiles_over", [P, T])
        tiles_used = sb("tiles_used", [P, 1])
        span = sb("span", [P, 3])
        span_int = [sb(f"span_int{p}", [P, 3], I32) for p in range(2)]
        list_vals = sb("list_vals", [P, 2])
        list_skip = sb("list_skip", [P, 1])
        first_row = sb("first_row", [P, 2])
        medium_load = [sb(f"medium_load{p}", [P, 1], U32) for p in range(2)]
        medium_self = [sb(f"medium_self{p}", [P, 1], U32) for p in range(2)]
        medium_store = [sb(f"medium_store{p}", [P, 1], U32) for p in range(2)]
        dense_load = sb("dense_load", [P, 1], U32)
        inv_degree = sb("inv_degree", [P, T])
        dense_store = sb("dense_store", [P, 1], U32)
        long_adj = sb("long_adj", [P, N])
        long_x = sb("long_x", [P, F])
        weights = [sb(f"weights{k}", [P, N]) for k in range(2)]
        xT = weights[0][0:F, :]
        row_max = sb("row_max", [P, HEADS])
        row_lrelu = sb("row_lrelu", [P, HEADS])
        neg_max = sb("neg_max", [P, HEADS])
        row_sum = sb("row_sum", [P, HEADS])
        row_rcp = sb("row_rcp", [P, HEADS])
        long_a = sb("long_a", [P, 1, F])
        long_b = sb("long_b", [P, 1, F])
        long_sq = sb("long_sq", [P, 1, F])
        long_stat = sb("long_stat", [P, 4])
        long_x1 = sb("long_x1", [P, F])
        prod = sb("prod", [P, AS * F])
        onehot = prod[:, 0:T * P // 2].bitcast(F16).rearrange("p (t e) -> p t e", t=T)
        weightsT = prod[:, T * P // 2:T * P // 2 + T * P].rearrange("p (t e) -> p t e", t=T)
        otherT = prod[:, T * P // 2 + T * P:T * P // 2 + T * P + N]
        merged = prod[:, T * F:2 * T * F].rearrange("p (t f) -> p t f", t=T)
        score = sb("score", [P, AS * HEADS])
        lrelu = sb("lrelu", [P, AS * HEADS])
        slot_max = sb("slot_max", [P, (T + 1) * HEADS])
        expw = score
        den = sb("den", [P, (T + 1) * HEADS])
        u = sb("u", [P, T + 1, F])
        uc = sb("uc", [P, T + 1, F])
        sq = sb("sq", [P, T + 1, F])
        dense_xT = sq[0:F, 0:2, :].rearrange("p t f -> p (t f)")
        dense_selfT = sq[:, 2:4, :].rearrange("p t f -> p (t f)")
        stat = sb("stat", [P, 4, T + 1])
        x1 = sb("x1", [P, T + 1, F])
        x1_parts = sb("x1_parts", [P, T, 3, F], BF16)
        y = uc[:, 0:T, :]
        ident = sb("ident", [P, P])
        w_all = sb("w_all", [F, C])
        w_self_pad = sb("w_self_pad", [F, P])
        w_other_pad = sb("w_other_pad", [F, P])
        bias_bc = sb("bias_bc", [P, HO])
        key_iota = sb("key_iota", [P, T])
        key_mat = sb("key_mat", [P, T, P + 1], F16)
        before = sb("before", [P, P], F16)
        ones = sb("ones", [P, P], F16)
        col_iota = sb("col_iota", [P, P])
        row_names = sb("row_names", [P, T, 2], F16)
        tile_steps = sb("tile_steps", [P, T])
        zero_row = sb("zero_row", [P, T])

        ring = ps("ring", [P, 4, 512])
        mid = ps("mid", [P, 3, 512])
        misc = ps("misc", [P, 512])
        rank_ps = misc[:, 0:3 * T]
        list_ps = misc[:, 48:50]
        long_out = misc[:, 64:64 + HO]
        long_xT_ps = misc[0:F, 128:256]
        long_selfT_ps = misc[:, 256:384]

        weights_in, const_ready, cleared, key_mat_ready, first_contents, psum_cleared = (
            sem("weights_in"), sem("const_ready"), sem("cleared"), sem("key_mat_ready"), sem("first_contents"),
            sem("psum_cleared"))
        scratch_init, pad_ready, mask_ready = sem("scratch_init"), sem("pad_ready"), sem("mask_ready")
        x_loaded = [sem(f"x_loaded{p}") for p in range(2)]
        xT_ps_ready, xT_ready = sem("xT_ps_ready"), sem("xT_ready")
        proj_ps_ready, proj_ready = sem("proj_ps_ready"), sem("proj_ready")
        table_written = [sem(f"table_written{p}") for p in range(2)]
        adj_loaded = [sem(f"adj_loaded{s}") for s in range(4)]
        adj_transposed = sem("adj_transposed")
        adjT_by_act, adjT_by_dve = sem("adjT_by_act"), sem("adjT_by_dve")
        keys_ps_ready, keys_taken, index_ready = sem("keys_ps_ready"), sem("keys_taken"), sem("index_ready")
        extract_step, long16_ready, rank_ps_ready, span_ready = (
            sem("extract_step"), sem("long16_ready"), sem("rank_ps_ready"), sem("span_ready"))
        medium_list = [sem(f"medium_list_{s}") for s in ("onehot", "ps", "step", "ready")]
        dense_list = [sem(f"dense_list_{s}") for s in ("onehot", "ps", "step", "ready")]
        medium_adj_loaded, medium_rows_loaded, medium_step, medium_index_ready = (
            sem("medium_adj_loaded"), sem("medium_rows_loaded"), sem("medium_step"), sem("medium_index_ready"))
        medium_slots_loaded, medium_x1_ready, medium_stored = (
            sem("medium_slots_loaded"), sem("medium_x1_ready"), sem("medium_stored"))
        dense16_ready, dense_rank_ps_ready, dense_rank_step, rank_moved = (
            sem("dense16_ready"), sem("dense_rank_ps_ready"), sem("dense_rank_step"), sem("rank_moved"))
        dense_xT_ps_ready, dense_xT_ready = sem("dense_xT_ps_ready"), sem("dense_xT_ready")
        otherT_ps_ready, otherT_ready = sem("otherT_ps_ready"), sem("otherT_ready")
        dense_tile_over, dense_over = sem("dense_tile_over"), sem("dense_over")
        slots_loaded = [sem(f"slots_loaded{p}") for p in range(2)]
        attend_step, exp_in_ready, exp_ready, gathered_read = (
            sem("attend_step"), sem("exp_in_ready"), sem("exp_ready"), sem("gathered_read"))
        centred, squared, var_ready, rstd_ready, ln_ready = (
            sem("centred"), sem("squared"), sem("var_ready"), sem("rstd_ready"), sem("ln_ready"))
        part_in_ready, part_ready, parts_ready = sem("part_in_ready"), sem("part_ready"), sem("parts_ready")
        long_loaded, long_xT_ps_ready, long_xT_ready = sem("long_loaded"), sem("long_xT_ps_ready"), sem("long_xT_ready")
        selfT_ps_ready, selfT_ready = sem("selfT_ps_ready"), sem("selfT_ready")
        long_step, scores_ready, scores_read, neg_max_ready = (
            sem("long_step"), sem("scores_ready"), sem("scores_read"), sem("neg_max_ready"))
        weights_ready, weights_transposed = sem("weights_ready"), sem("weights_transposed")
        weightsT_by_dve, weightsT_by_act, long_out_ready = (
            sem("weightsT_by_dve"), sem("weightsT_by_act"), sem("long_out_ready"))
        long_centred, long_squared, long_var, long_ln, long_rstd = (
            sem("long_centred"), sem("long_squared"), sem("long_var"), sem("long_ln"), sem("long_rstd"))
        long_x1_ready, long_stored = sem("long_x1_ready"), sem("long_stored")
        merged_loaded = [sem(f"merged_loaded{p}") for p in range(2)]
        agg_ps_ready, agg_read, agg_step, agg_done, y_ready, y_stored = (
            sem("agg_ps_ready"), sem("agg_read"), sem("agg_step"), sem("agg_done"), sem("y_ready"), sem("y_stored"))

        class Batch:

            def __init__(self, j, p, r):
                self.j, self.p, self.r = j, p, r

        AGG0, ATTEND0, LONG0, Y0 = T // 2 + 1, 2, 1, 1
        RING0, RING_ACT0, RING_DVE0 = 12, 4, 2
        starts = ((agg_ps_ready, AGG0), (agg_read, AGG0), (gathered_read, ATTEND0), (parts_ready, ATTEND0),
                  (long_out_ready, LONG0), (scores_read, LONG0), (weightsT_by_act, LONG0), (weightsT_by_dve, LONG0),
                  (dense_tile_over, LONG0), (y_stored, Y0), (adj_transposed, RING0), (adjT_by_act, RING_ACT0),
                  (adjT_by_dve, RING_DVE0))
        wait_passed = {e: sem(f"wait_passed_{e}") for e in ("Pool", "Activation", "PE", "DVE", "SP")}

        def alone(eng):
            eng.sem_inc(wait_passed[str(eng.engine).split(".")[-1]], 1)

        def chain(eng, semaphore, base):
            count = [0]

            def step(instruction):
                count[0] += 1
                instruction.then_inc(semaphore, 1)
                eng.wait_ge(semaphore, base + count[0])
            step.count = lambda: count[0]
            return step

        def pipeline(extract, rest, eng):
            with eng.Fori(0, B // 2 - 1) as k:
                batches = Batch(2 * k, 0, k), Batch(2 * k + 1, 1, k), Batch(2 * k + 2, 0, k + 1)
                for b, next_b in zip(batches[:2], batches[1:]):
                    extract(next_b)
                    rest(b, next_b)
            b, next_b = Batch(B - 2, 0, B // 2 - 1), Batch(B - 1, 1, B // 2 - 1)
            extract(next_b)
            rest(b, next_b)
            rest(next_b, None)

        def load_span(eng, b):
            eng.wait_ge(span_ready, b.j + 1)
            alone(eng)
            first = eng.value_load(span_int[b.p][0:1, 0:1], min_val=0, max_val=B * T)
            end = eng.value_load(span_int[b.p][0:1, 1:2], min_val=0, max_val=B * T)
            batches = eng.value_load(span_int[b.p][0:1, 2:3], min_val=0, max_val=B)
            return first, end, batches

        def row_dmas(eng, dram, j, tile, store, semaphore):
            for rows, count, t0, t1 in ((0, P, 0, T - 1), (P * (T - 1), LAST16, T - 1, T),
                                        (P * (T - 1) + LAST16, LAST - LAST16, T - 1, T)):
                side = dram[bass.ds(j, 1), rows:rows + (t1 - t0) * count, :].rearrange(
                    "o (t p) f -> p (o t) f", p=count)
                at = rows % P
                part = tile[at:at + count, t0:t1, :]
                src, dst = (part, side) if store else (side, part)
                eng.dma_start(dst, src).then_inc(semaphore, 16)

        block = ctx.enter_context(nc.Block())

        @block.sync
        def _(sp):
            for dst, w in ((w_all[:, 0:F], w_self), (w_all[:, F:2 * F], w_other), (w_all[:, 2 * F:C], w_feat)):
                sp.dma_start(dst.rearrange("f (h o) -> f h o", h=HEADS),
                             w.rearrange("h f o -> f h o")).then_inc(weights_in, 16)
            sp.wait_ge(pad_ready, 3)
            for dst, w in ((w_self_pad, w_self), (w_other_pad, w_other)):
                sp.dma_start(dst[:, :].rearrange("f (h o) -> f h o", h=HEADS)[:, :, 0:ATT],
                             w.rearrange("h f o -> f h o")).then_inc(weights_in, 16)
            sp.dma_start(bias_bc[:, :], bias.rearrange("a b h o -> (a b) (h o)").broadcast_to([P, HO])
                         ).then_inc(weights_in, 16)

            def load_x(b):
                row_dmas(sp, x, b.j, x_in[b.p], False, x_loaded[b.p])

            def load_adj(b, tiles):
                for t in tiles:
                    s = t % 4
                    sp.wait_ge(adj_transposed, RING0 + 3 * (T * b.j + t - 3))
                    for r0, r1 in ((0, P),) if t < T - 1 else ((0, LAST16), (LAST16, LAST)):
                        sp.dma_start(adj_in[r0:r1, s, :], adj[bass.ds(b.j, 1), P * t + r0:P * t + r1, :].rearrange(
                            "o p m -> p (o m)")).then_inc(adj_loaded[s], 16)

            def load_rest(b):
                load_adj(b, range(4, 8))
                sp.wait_ge(proj_ready, (T // 2) * (b.j + 1))
                sp.wait_ge(parts_ready, ATTEND0 + b.j - 1)
                for dst, c0, c1 in ((table[b.p], F, C), (self_table[b.p], 0, F)):
                    for r0, r1, t0, t1 in ((0, P, 0, T - 1), (0, LAST16, T - 1, T), (LAST16, LAST, T - 1, T)):
                        row0 = P * t0 + r0
                        rows = dst[row0:row0 + (r1 - r0) * (t1 - t0), :].rearrange("(t p) f -> p t f", p=r1 - r0)
                        sp.dma_start(rows, proj[b.p][r0:r1, t0:t1, c0:c1]).then_inc(table_written[b.p], 16)
                load_adj(b, range(8, T))

            def read_back(b):
                sp.wait_ge(medium_stored, 16 * (b.j + 1))
                sp.wait_ge(dense_over, b.j + 1)
                sp.dma_start(merged[:, :, :], long_x1_dram[b.p].rearrange("(t p) f -> p t f", p=P)
                             ).then_inc(merged_loaded[b.p], 16)

            def store_y(b):
                sp.wait_ge(y_ready, b.j + 1)
                row_dmas(sp, out, b.j, y, True, y_stored)

            def step(b, next_b, after_next):
                if next_b:
                    load_rest(next_b)
                if after_next:
                    load_adj(after_next, range(4))
                read_back(b)
                if after_next:
                    sp.wait_ge(parts_ready, ATTEND0 + b.j + 1)
                    load_x(after_next)
                store_y(b)

            batch0, batch1 = Batch(0, 0, 0), Batch(1, 1, 0)
            load_x(batch0)
            load_x(batch1)
            load_adj(batch0, range(4))
            sp.wait_ge(cleared, 1)
            for p in range(2):
                sp.dma_start(long_x1_dram[p].rearrange("(p a) f -> p (a f)", p=P),
                             sq[:, 0:T, :].rearrange("p t f -> p (t f)")).then_inc(scratch_init, 16)
            load_rest(batch0)
            load_adj(batch1, range(4))
            with sp.Fori(0, B // 2 - 1) as k:
                step(Batch(2 * k, 0, k), Batch(2 * k + 1, 1, k), Batch(2 * k + 2, 0, k + 1))
                step(Batch(2 * k + 1, 1, k), Batch(2 * k + 2, 0, k + 1), Batch(2 * k + 3, 1, k + 1))
            step(Batch(B - 2, 0, B // 2 - 1), Batch(B - 1, 1, B // 2 - 1), None)
            step(Batch(B - 1, 1, B // 2 - 1), None, None)
            sp.wait_ge(y_stored, Y0 + 48 * B)

        @block.gpsimd
        def _(pool):
            for semaphore, count in starts:
                pool.sem_inc(semaphore, count)
            pool.memset(w_self_pad[:, :], 0.0)
            pool.memset(w_other_pad[:, :], 0.0).then_inc(pad_ready, 1)
            for p in range(2):
                pool.memset(x_in[p][:, T - 1, :], 0.0).then_inc(pad_ready, 1)
            pool.memset(sq[:, :, :], 0.0).then_inc(cleared, 1)
            pool.memset(ident[:, :], 0.0).then_inc(mask_ready, 1)
            pool.memset(before[:, :], 1.0).then_inc(mask_ready, 1)
            pool.memset(ones[:, :], 1.0).then_inc(const_ready, 1)
            pool.memset(row_names[:, :, 1:2], 1.0).then_inc(const_ready, 1)
            pool.iota(key_iota[:, :], pattern=[[P, T]], base=1, channel_multiplier=1,
                      allow_small_or_imprecise_dtypes=True).then_inc(const_ready, 1)
            pool.iota(col_iota[:, :], pattern=[[1, P]], base=0, channel_multiplier=0,
                      allow_small_or_imprecise_dtypes=True).then_inc(const_ready, 1)
            pool.iota(row_names[:, :, 0:1], pattern=[[P, T]], base=0, channel_multiplier=1,
                      allow_small_or_imprecise_dtypes=True).then_inc(const_ready, 1)
            pool.iota(tile_steps[:, :], pattern=[[P, T]], base=0, channel_multiplier=0,
                      allow_small_or_imprecise_dtypes=True).then_inc(const_ready, 1)
            pool.iota(node_iota[:, :], pattern=[[1, N]], base=1, channel_multiplier=0,
                      allow_small_or_imprecise_dtypes=True).then_inc(const_ready, 1)
            pool.wait_ge(mask_ready, 2)
            pool.affine_select(out=ident[:, :], in_=ident[:, :], compare_op=ALU.not_equal, fill=1.0,
                               base=0, pattern=[[-1, P]], channel_multiplier=1).then_inc(const_ready, 1)
            pool.affine_select(out=before[:, :], in_=before[:, :], compare_op=ALU.is_gt, fill=0.0,
                               base=0, pattern=[[1, P]], channel_multiplier=-1).then_inc(const_ready, 1)
            pool.memset(gathered[0][:, :, :, :], 0.0).then_inc(cleared, 1)
            pool.memset(gathered[1][:, :, :, :], 0.0).then_inc(cleared, 1)
            pool.memset(medium_gathered[:, :, :], 0.0).then_inc(cleared, 1)

            def gather_slots(b, groups):
                if groups[0] == 0:
                    pool.wait_ge(table_written[b.p], 96 * (b.r + 1))
                    pool.wait_ge(gathered_read, ATTEND0 + b.j - 1)
                for g in groups:
                    pool.wait_ge(index_ready, GROUPS * b.j + g + 1)
                    alone(pool)
                    for t in range(3 * g, 3 * g + 3):
                        for s in range(SLOTS):
                            pool.indirect_dma_start(
                                gathered[b.p][0:ROWS[t], t, s, :], None, table[b.p],
                                bass.IndirectOffsetOnAxis(ap=index[b.p][0:ROWS[t], t, s:s + 1], axis=0),
                                bounds_check=N - 1, oob_is_err=False).then_inc(slots_loaded[b.p], 16)

            def gather(dst, src, index, rows, semaphore):
                pool.indirect_dma_start(dst, None, src, bass.IndirectOffsetOnAxis(ap=index, axis=0),
                                        bounds_check=rows - 1, oob_is_err=False).then_inc(semaphore, 16)

            def scatter(b, src, index, semaphore):
                pool.indirect_dma_start(long_x1_dram[b.p], bass.IndirectOffsetOnAxis(ap=index, axis=0), src, None,
                                        bounds_check=T * P - 1, oob_is_err=False).then_inc(semaphore, 16)

            def load_medium(b):
                pool.wait_ge(medium_list[3], b.j + 1)
                alone(pool)
                gather(long_adj[:, :], adj_rows, medium_load[b.p][:, 0:1], B * N, medium_adj_loaded)
                gather(x_in[b.p][:, T, :], x_rows, medium_load[b.p][:, 0:1], B * N, medium_rows_loaded)
                gather(proj[b.p][:, T, 0:F], self_table[b.p], medium_self[b.p][:, 0:1], N, medium_rows_loaded)

            def gather_medium_slots(b):
                pool.wait_ge(medium_index_ready, b.j + 1)
                pool.wait_ge(gathered_read, ATTEND0 + b.j)
                alone(pool)
                for s in range(MSLOTS):
                    gather(medium_gathered[:, s, :], table[b.p], medium_index[:, s:s + 1], N, medium_slots_loaded)

            def store_medium(b):
                pool.wait_ge(medium_x1_ready, b.j + 1)
                alone(pool)
                scatter(b, x1[:, T, :], medium_store[b.p][:, 0:1], medium_stored)

            def dense(b):
                first, end, _ = load_span(pool, b)
                with pool.If(end - first > 0):
                    with pool.Fori(first, end) as q:
                        pool.wait_ge(dense_list[3], q + 1)
                        alone(pool)
                        gather(long_adj[:, :], adj_rows, dense_load[:, 0:1], B * N, long_loaded)
                        gather(long_x[:, :], x_rows, dense_load[:, 0:1], B * N, long_loaded)
                        pool.wait_ge(long_x1_ready, q + 1)
                        alone(pool)
                        scatter(b, long_x1[:, :], dense_store[:, 0:1], long_stored)
                        pool.wait_ge(long_stored, 16 * (q + 1))
                        pool.sem_inc(dense_tile_over, 1)
                pool.sem_inc(dense_over, 1)

            def next_batch(b, done):
                gather_slots(b, [0, 1])
                dense(done)
                load_medium(b)
                gather_slots(b, [2, 3])
                store_medium(done)
                gather_medium_slots(b)

            batch0 = Batch(0, 0, 0)
            pool.wait_ge(scratch_init, 32)
            pool.wait_ge(cleared, 4)
            gather_slots(batch0, range(GROUPS))
            load_medium(batch0)
            gather_medium_slots(batch0)
            with pool.Fori(0, B // 2 - 1) as k:
                next_batch(Batch(2 * k + 1, 1, k), Batch(2 * k, 0, k))
                next_batch(Batch(2 * k + 2, 0, k + 1), Batch(2 * k + 1, 1, k))
            next_batch(Batch(B - 1, 1, B // 2 - 1), Batch(B - 2, 0, B // 2 - 1))
            last = Batch(B - 1, 1, B // 2 - 1)
            dense(last)
            store_medium(last)

        @block.tensor
        def _(pe):
            pe.wait_ge(weights_in, 16 * 6)
            pe.wait_ge(const_ready, 9)
            pe.wait_ge(key_mat_ready, 1)
            pe.wait_ge(psum_cleared, 1)

            def project(b):
                pe.wait_ge(agg_read, AGG0 + (T // 2) * (b.j - 1))
                pe.wait_ge(x_loaded[b.p], 48 * (b.r + 1))
                alone(pe)
                for t in range(T):
                    last = pe.transpose(mid[0:F, t // 4, P * (t % 4):P * (t % 4) + ROWS[t]],
                                        x_in[b.p][0:ROWS[t], t, :], ident[0:ROWS[t], 0:ROWS[t]])
                    if t % 4 == 3:
                        last.then_inc(xT_ps_ready, 1)
                for g in range(T // 2):
                    if g < 3:
                        pe.wait_ge(xT_ready, 3 * b.j + g + 1)
                    else:
                        pe.wait_ge(proj_ready, (T // 2) * b.j + g - 2)
                    for t in (2 * g, 2 * g + 1):
                        pe.wait_ge(xT_ready, 3 * b.j + t // 4 + 1)
                        last = pe.matmul(mid[0:ROWS[t], g % 3, 256 * (t % 2):256 * (t % 2) + C],
                                         xT[:, P * t:P * t + ROWS[t]], w_all[:, :], start=True, stop=True)
                    last.then_inc(proj_ps_ready, 1)

            def transpose_tile(b, t):
                s = t % 4
                more = 16 if t == T - 1 else 0
                loads = 64 if s == 3 else 48
                pe.wait_ge(adj_loaded[s], loads * b.j + 16 * (t // 4 + 1) + more)
                for k in range(3):
                    v = 3 * t + k - 4
                    tt, kk = v // 3, v % 3
                    if kk == 2:
                        pe.wait_ge(adjT_by_dve, RING_DVE0 + T * b.j + tt + 1)
                    else:
                        pe.wait_ge(adjT_by_act, RING_ACT0 + 2 * T * b.j + 2 * tt + kk + 1)
                    for c in range(4 * k, 4 * k + 4):
                        last = pe.transpose(ring[0:ROWS[c], (3 * t + k) % 4, P * (c % 4):P * (c % 4) + ROWS[t]],
                                            adj_in[0:ROWS[t], s, P * c:P * c + ROWS[c]],
                                            ident[0:ROWS[t], 0:ROWS[t]])
                    last.then_inc(adj_transposed, 1)

            def keys_of_tile(b, t):
                g = t // 3
                if t % 3 == 0:
                    if g < 3:
                        pe.wait_ge(proj_ready, (T // 2) * b.j + 3 + g + 1)
                    else:
                        pe.wait_ge(keys_taken, GROUPS * b.j + g - 2)
                pe.wait_ge(adjT_by_act, RING_ACT0 + 2 * T * b.j + 2 * t + 2)
                pe.wait_ge(adjT_by_dve, RING_DVE0 + T * b.j + t + 1)
                alone(pe)
                for c in range(T):
                    last = pe.matmul(mid[0:ROWS[t], g % 3, (P + 1) * (t % 3):(P + 1) * (t % 3 + 1)],
                                     adjT[b.p][0:ROWS[c], c, P * t:P * t + ROWS[t]],
                                     key_mat[0:ROWS[c], c, :], start=(c == 0), stop=(c == T - 1))
                if t % 3 == 2:
                    last.then_inc(keys_ps_ready, 1)

            def list_rows(sems, count):
                pe.wait_ge(sems[0], count)
                for t in range(T):
                    last = pe.matmul(list_ps, onehot[:, t, :], row_names[:, t, :],
                                     start=(t == 0), stop=(t == T - 1))
                last.then_inc(sems[1], 1)

            def extract(b):
                project(b)
                for t in range(T):
                    transpose_tile(b, t)
                    if t > 0:
                        keys_of_tile(b, t - 1)
                keys_of_tile(b, T - 1)
                pe.wait_ge(long16_ready, b.j + 1)
                pe.matmul(rank_ps[:, 0:T], before[:, :], long16[:, 0:T], start=True, stop=True)
                pe.matmul(rank_ps[:, T:3 * T], ones[:, :], long16[:, :], start=True, stop=True
                          ).then_inc(rank_ps_ready, 1)
                list_rows(medium_list, b.j + 1)

            def long_scores(b, q, h):
                pe.wait_ge(scores_read, LONG0 + HEADS * q + h)
                for c in range(3):
                    cols = min(512, N - 512 * c)
                    last = pe.matmul(mid[:, c, 0:cols], dense_selfT[32 * h:32 * h + ATT, :],
                                     otherT[32 * h:32 * h + ATT, 512 * c:512 * c + cols],
                                     start=True, stop=True)
                last.then_inc(scores_ready, 1)

            def long_transposes(q, h):
                pe.wait_ge(weights_ready, HEADS * q + h + 1)
                for k in range(3):
                    if k < 2:
                        pe.wait_ge(weightsT_by_dve, LONG0 + 2 * (HEADS * q + h))
                    else:
                        pe.wait_ge(weightsT_by_act, LONG0 + HEADS * q + h)
                    for c in range(4 * k, 4 * k + 4):
                        last = pe.transpose(ring[0:ROWS[c], k, P * (c % 4):P * (c % 4) + P],
                                            weights[h % 2][:, P * c:P * c + ROWS[c]], ident[:, :])
                    last.then_inc(weights_transposed, 1)

            def long_products(b, q, h):
                pe.wait_ge(weightsT_by_dve, LONG0 + 2 * (HEADS * q + h + 1))
                pe.wait_ge(weightsT_by_act, LONG0 + HEADS * q + h + 1)
                for c in range(T):
                    last = pe.matmul(long_out[:, OUT * h:OUT * (h + 1)], weightsT[0:ROWS[c], c, :],
                                     proj[b.p][0:ROWS[c], c, 2 * F + OUT * h:2 * F + OUT * (h + 1)],
                                     start=(c == 0), stop=(c == T - 1))
                last.then_inc(long_out_ready, 1)

            def long_tile(b, q):
                pe.wait_ge(long_loaded, 32 * (q + 1))
                alone(pe)
                pe.transpose(long_xT_ps, long_x[:, :], ident[:, :]).then_inc(long_xT_ps_ready, 1)
                pe.wait_ge(long_xT_ready, q + 1)
                pe.matmul(long_selfT_ps, w_self_pad[:, :], dense_xT[:, :], start=True, stop=True
                          ).then_inc(selfT_ps_ready, 1)
                pe.wait_ge(selfT_ready, q + 1)
                long_scores(b, q, 0)
                for h in range(HEADS):
                    if h + 1 < HEADS:
                        long_scores(b, q, h + 1)
                    long_transposes(q, h)
                    long_products(b, q, h)

            def prepare_dense(b, d):
                pe.wait_ge(dense16_ready, d + 1)
                pe.matmul(rank_ps[:, 0:T], before[:, :], dense16[:, :], start=True, stop=True)
                pe.matmul(rank_ps[:, T:2 * T], ones[:, :], dense16[:, :], start=True, stop=True
                          ).then_inc(dense_rank_ps_ready, 1)
                for t in range(T):
                    last = pe.transpose(mid[0:F, t // 4, P * (t % 4):P * (t % 4) + ROWS[t]],
                                        x_in[b.p][0:ROWS[t], t, :], ident[0:ROWS[t], 0:ROWS[t]])
                    if t % 4 == 3:
                        last.then_inc(dense_xT_ps_ready, 1)
                for c in range(3):
                    pe.wait_ge(dense_xT_ready, 3 * d + c + 1)
                    cols = min(512, N - 512 * c)
                    pe.matmul(mid[:, c, 0:cols], w_other_pad[:, :], xT[:, 512 * c:512 * c + cols],
                              start=True, stop=True).then_inc(otherT_ps_ready, 1)
                pe.wait_ge(otherT_ready, 3 * d + 3)

            def rest(b, next_b):
                extracted = (next_b or b).j + 1
                pe.wait_ge(adjT_by_act, RING_ACT0 + 2 * T * extracted)
                pe.wait_ge(adjT_by_dve, RING_DVE0 + T * extracted)
                pe.wait_ge(keys_taken, GROUPS * extracted)
                pe.wait_ge(medium_list[3], extracted)
                first, end, batches = load_span(pe, b)
                with pe.If(end - first > 0):
                    prepare_dense(b, batches)
                    alone(pe)
                    with pe.Fori(first, end) as q:
                        list_rows(dense_list, q + 1)
                        pe.wait_ge(dense_list[3], q + 1)
                        long_tile(b, q)
                pe.wait_ge(weightsT_by_dve, LONG0 + 2 * HEADS * end)
                pe.wait_ge(weightsT_by_act, LONG0 + HEADS * end)
                pe.wait_ge(scores_read, LONG0 + HEADS * end)
                pe.wait_ge(parts_ready, ATTEND0 + b.j + 1)
                for t in range(T):
                    g = t // 2
                    if t % 2 == 0 and g >= 3:
                        pe.wait_ge(agg_read, AGG0 + (T // 2) * b.j + g - 2)
                    if t % 2 == 0 and (g == 0 or g >= 3):
                        alone(pe)
                    for c in range(T):
                        last = pe.matmul(mid[0:ROWS[t], g % 3, 256 * (t % 2):256 * (t % 2) + 3 * F],
                                         adjT[b.p][0:ROWS[c], c, P * t:P * t + ROWS[t]],
                                         x1_parts[0:ROWS[c], c, :, :].rearrange("p a f -> p (a f)"),
                                         start=(c == 0), stop=(c == T - 1))
                    if t % 2 == 1:
                        last.then_inc(agg_ps_ready, 1)

            extract(Batch(0, 0, 0))
            pipeline(extract, rest, pe)

        @block.scalar
        def _(act):
            act.wait_ge(scratch_init, 32)

            def extract(b):
                for u3 in range(3):
                    act.wait_ge(xT_ps_ready, 3 * b.j + u3 + 1)
                    cols = min(512, N - 512 * u3)
                    act.copy(xT[:, 512 * u3:512 * u3 + cols], mid[0:F, u3, 0:cols]).then_inc(xT_ready, 1)
                act.wait_ge(parts_ready, ATTEND0 + b.j - 1)
                for g in range(T // 2):
                    act.wait_ge(proj_ps_ready, (T // 2) * b.j + g + 1)
                    act.copy(proj[b.p][:, 2 * g:2 * g + 2, :],
                             mid[:, g % 3, :].rearrange("p (t c) -> p t c", t=2)[:, :, 0:C]
                             ).then_inc(proj_ready, 1)
                act.wait_ge(agg_ps_ready, AGG0 + (T // 2) * (b.j - 1))
                for t in range(T):
                    for k in range(2):
                        act.wait_ge(adj_transposed, RING0 + 3 * (T * b.j + t) + k + 1)
                        alone(act)
                        act.copy(adjT[b.p][:, 4 * k:4 * k + 4, P * t:P * t + ROWS[t]],
                                 ring[:, (3 * t + k) % 4, :].rearrange("p (c n) -> p c n", c=4)[:, :, 0:ROWS[t]],
                                 saturate=False).then_inc(adjT_by_act, 1)

            def long_tile(b, q):
                act.wait_ge(long_xT_ps_ready, q + 1)
                act.copy(dense_xT[:, :], long_xT_ps).then_inc(long_xT_ready, 1)
                act.wait_ge(selfT_ps_ready, q + 1)
                act.copy(dense_selfT[:, :], long_selfT_ps).then_inc(selfT_ready, 1)
                for h in range(HEADS):
                    n = HEADS * q + h
                    act.wait_ge(neg_max_ready, n + 1)
                    act.activation(weights[h % 2][:, :], weights[h % 2][:, :], ACT.Exp,
                                   bias=neg_max[:, h:h + 1], scale=SCALE,
                                   accum_out=row_sum[:, h:h + 1]).then_inc(weights_ready, 1)
                    act.wait_ge(weights_transposed, 3 * n + 3)
                    act.wait_ge(long_out_ready, LONG0 + n)
                    act.copy(weightsT[:, 8:12, :], ring[:, 2, :].rearrange("p (c n) -> p c n", c=4)
                             ).then_inc(weightsT_by_act, 1)
                act.wait_ge(long_centred, q + 1)
                act.activation(long_sq[:, :, :], long_b[:, :, :], ACT.Square).then_inc(long_squared, 1)
                act.wait_ge(long_var, q + 1)
                act.activation(long_stat[:, 2:3], long_stat[:, 1:2], ACT.Ln).then_inc(long_ln, 1)
                act.wait_ge(long_ln, q + 1)
                act.activation(long_stat[:, 3:4], long_stat[:, 2:3], ACT.Exp, scale=-0.5).then_inc(long_rstd, 1)

            def layernorm(n, tiles):
                act.wait_ge(centred, n)
                act.activation(sq[:, 0:tiles, :], uc[:, 0:tiles, :], ACT.Square).then_inc(squared, 1)
                act.wait_ge(var_ready, n)
                act.activation(stat[:, 2, 0:tiles], stat[:, 1, 0:tiles], ACT.Ln).then_inc(ln_ready, 1)
                act.wait_ge(ln_ready, n)
                act.activation(stat[:, 3, 0:tiles], stat[:, 2, 0:tiles], ACT.Exp, scale=-0.5).then_inc(rstd_ready, 1)

            def prepare_dense(d):
                for c in range(3):
                    act.wait_ge(dense_xT_ps_ready, 3 * d + c + 1)
                    cols = min(512, N - 512 * c)
                    act.copy(xT[:, 512 * c:512 * c + cols], mid[0:F, c, 0:cols]).then_inc(dense_xT_ready, 1)
                for c in range(3):
                    act.wait_ge(otherT_ps_ready, 3 * d + c + 1)
                    cols = min(512, N - 512 * c)
                    act.copy(otherT[:, 512 * c:512 * c + cols], mid[:, c, 0:cols]).then_inc(otherT_ready, 1)

            def rest(b, next_b):
                first, end, batches = load_span(act, b)
                with act.If(end - first > 0):
                    prepare_dense(batches)
                    with act.Fori(first, end) as q:
                        long_tile(b, q)
                act.wait_ge(exp_in_ready, b.j + 1)
                act.activation(expw[:, :], score[:, :], ACT.Exp, scale=SCALE).then_inc(exp_ready, 1)
                layernorm(2 * b.j + 1, T + 1)
                act.wait_ge(part_in_ready, 2 * b.j + 1)
                act.wait_ge(agg_ps_ready, AGG0 + (T // 2) * b.j)
                act.copy(x1_parts[:, :, 0, :], x1[:, 0:T, :]).then_inc(part_ready, 1)
                act.wait_ge(part_in_ready, 2 * b.j + 2)
                act.copy(x1_parts[:, :, 1, :], u[:, 0:T, :]).then_inc(part_ready, 1)
                layernorm(2 * b.j + 2, T)

            extract(Batch(0, 0, 0))
            pipeline(extract, rest, act)

        @block.vector
        def _(dve):
            dve.memset(ring[:, :, :], 0.0)
            dve.memset(mid[:, :, :], 0.0)
            dve.memset(misc[:, :], 0.0).then_inc(psum_cleared, 1)
            for p in range(2):
                dve.memset(degree[p][:, :], 0.0)
                dve.memset(first_row[:, p:p + 1], float(N * (p - 2)))
            dve.memset(keys[:, :, :], 0.0)
            dve.memset(zero_row[:, :], 0.0)
            dve.memset(span[:, :], 0.0)
            dve.memset(tiles_over[:, :], 0.0)
            dve.memset(key_mat[:, :, P:P + 1], 1.0).then_inc(first_contents, 1)
            dve.wait_ge(first_contents, 1)
            dve.wait_ge(const_ready, 9)
            dve.tensor_tensor(key_mat[:, :, 0:P], ident[:, :].unsqueeze(1).broadcast_to([P, T, P]),
                              key_iota[:, :].unsqueeze(2).broadcast_to([P, T, P]), ALU.mult
                              ).then_inc(key_mat_ready, 1)
            dve.wait_ge(key_mat_ready, 1)
            dve.wait_ge(weights_in, 16 * 6)

            def make_list(b, sems, count, load, store, row=None):
                one_sem, ps_sem, step_sem, ready_sem = sems
                step = chain(dve, step_sem, STEPS_LIST * (count - 1))
                dve.tensor_tensor(onehot[:, :, :], rank[b.p][:, :].unsqueeze(2).broadcast_to([P, T, P]),
                                  col_iota[:, :].unsqueeze(1).broadcast_to([P, T, P]), ALU.is_equal
                                  ).then_inc(one_sem, 1)
                dve.wait_ge(ps_sem, count)
                step(dve.tensor_copy(list_vals[:, :], list_ps))
                dve.tensor_scalar(load[:, :], list_vals[:, 0:1], first_row[:, b.p:b.p + 1], None, ALU.add)
                if row is not None:
                    dve.tensor_copy(row[:, :], list_vals[:, 0:1])
                step(dve.tensor_scalar(list_skip[:, :], list_vals[:, 1:2], -SKIP, SKIP, ALU.mult, ALU.add))
                dve.tensor_tensor(store[:, :], list_vals[:, 0:1], list_skip[:, :], ALU.add
                                  ).then_inc(ready_sem, 1)
                assert step.count() == STEPS_LIST

            def take_keys(b, g, step):
                dve.wait_ge(keys_ps_ready, GROUPS * b.j + g + 1)
                alone(dve)
                for t in range(3 * g, 3 * g + 3):
                    at = (P + 1) * (t % 3)
                    dve.max(keys[0:ROWS[t], t, :], mid[0:ROWS[t], g % 3, at:at + P])
                    last = dve.tensor_copy(degree[b.p][0:ROWS[t], t:t + 1], mid[0:ROWS[t], g % 3, at + P:at + P + 1])
                last.then_inc(keys_taken, 1)
                dve.wait_ge(keys_taken, GROUPS * b.j + g + 1)
                found = keys[:, 3 * g:3 * g + 3, 0:SLOTS]
                step(dve.tensor_scalar(index_skip[:, :, :], found, 0.5, SKIP, ALU.is_lt, ALU.mult))
                dve.scalar_tensor_tensor(index[b.p][:, 3 * g:3 * g + 3, :], found, -1.0, index_skip[:, :, :],
                                         ALU.add, ALU.add).then_inc(index_ready, 1)

            def extract(b):
                step = chain(dve, extract_step, STEPS_EXTRACT * b.j)
                step(dve.tensor_scalar(first_row[:, b.p:b.p + 1], first_row[:, b.p:b.p + 1], 2.0 * N, None, ALU.add))
                dve.wait_ge(agg_ps_ready, AGG0 + (T // 2) * (b.j - 1))
                for t in range(T):
                    dve.wait_ge(adj_transposed, RING0 + 3 * (T * b.j + t) + 3)
                    alone(dve)
                    chunk = ring[:, (3 * t + 2) % 4, :].rearrange("p (c n) -> p c n", c=4)
                    dve.tensor_copy(adjT[b.p][:, 8:12, P * t:P * t + ROWS[t]], chunk[:, :, 0:ROWS[t]],
                                    saturate=False).then_inc(adjT_by_dve, 1)
                    if t % 3 == 1 and t > 3:
                        take_keys(b, t // 3 - 1, step)
                take_keys(b, GROUPS - 1, step)

                kinds(b, step)
                assert step.count() == STEPS_EXTRACT

            def ranks(step, r, member):
                step(dve.tensor_tensor_scan(tile_end[:, :], rank_sums[:, T:2 * T], zero_row[:, :], 0.0,
                                            ALU.add, ALU.add))
                step(dve.scalar_tensor_tensor(r, member, -1.0e4, rank_sums[:, 0:T], ALU.mult, ALU.add))
                step(dve.scalar_tensor_tensor(r, r, 1.0e4, tile_end[:, :], ALU.add, ALU.add))
                step(dve.tensor_tensor(r, r, rank_sums[:, T:2 * T], ALU.subtract))

            def kinds(b, step):
                slots = valid[b.p][:, 0:TS].rearrange("p (t s) -> p t s", t=T)
                step(dve.tensor_scalar(slots, keys[:, :, 0:SLOTS], 0.5, None, ALU.is_gt))
                dve.tensor_scalar(penalty[b.p][:, 0:TS], valid[b.p][:, 0:TS], 1.0, BIG, ALU.subtract, ALU.mult)
                step(dve.tensor_reduce(key_found[:, :], slots, X, ALU.add))
                step(dve.tensor_tensor(is_long[b.p][:, :], key_found[:, :], degree[b.p][:, :], LONG_TEST))
                step(dve.scalar_tensor_tensor(is_medium[:, :], degree[b.p][:, :], MEDIUM_DEGREE + 0.5, is_long[b.p][:, :],
                                              ALU.is_lt, ALU.mult))
                step(dve.tensor_copy(long16[:, T:2 * T], is_long[b.p][:, :]))
                dve.tensor_copy(long16[:, 0:T], is_medium[:, :]).then_inc(long16_ready, 1)
                dve.wait_ge(rank_ps_ready, b.j + 1)
                step(dve.tensor_copy(rank_sums[:, :], rank_ps))
                ranks(step, rank[b.p][:, :], is_medium[:, :])
                step(dve.tensor_reduce(total_long[:, :], rank_sums[:, 2 * T:3 * T], X, ALU.add))
                step(dve.scalar_tensor_tensor(total_long[:, :], tile_end[:, T - 1:T], float(P), total_long[:, :],
                                              ALU.min, ALU.subtract))
                step(dve.tensor_scalar(total_long[:, :], total_long[:, :], -1.0, None, ALU.mult))
                step(dve.tensor_tensor(span[:, 2:3], span[:, 2:3], tiles_over[:, 0:1], ALU.add))
                step(dve.tensor_scalar(tiles_over[:, :], tile_steps[:, :], total_long[:, :], None, ALU.is_lt))
                step(dve.tensor_reduce(tiles_used[:, :], tiles_over[:, :], X, ALU.add))
                step(dve.tensor_copy(span[:, 0:1], span[:, 1:2]))
                step(dve.tensor_tensor(span[:, 1:2], span[:, 1:2], tiles_used[:, :], ALU.add))
                dve.tensor_copy(span_int[b.p][:, :], span[:, :]).then_inc(span_ready, 1)
                make_list(b, medium_list, b.j + 1, medium_load[b.p], medium_store[b.p], medium_self[b.p])

            def extract_medium(b):
                step = chain(dve, medium_step, STEPS_MEDIUM * b.j)
                dve.wait_ge(medium_adj_loaded, 16 * (b.j + 1))
                step(dve.tensor_tensor(long_adj[:, :], long_adj[:, :], node_iota[:, :], ALU.mult))
                alone(dve)
                step(dve.max(medium_keys[:, 0:8], long_adj[:, :]))
                alone(dve)
                step(dve.match_replace(long_adj[:, :], medium_keys[:, 0:8], long_adj[:, :], 0.0))
                alone(dve)
                step(dve.max(medium_keys[:, 8:16], long_adj[:, :]))
                found = medium_keys[:, 0:MSLOTS]
                step(dve.tensor_scalar(medium_skip[:, :], found, 0.5, SKIP, ALU.is_lt, ALU.mult))
                dve.scalar_tensor_tensor(medium_index[:, :], found, -1.0, medium_skip[:, :], ALU.add, ALU.add
                                         ).then_inc(medium_index_ready, 1)
                step(dve.tensor_scalar(valid[b.p][:, TS:AS], found, 0.5, None, ALU.is_gt))
                dve.tensor_scalar(penalty[b.p][:, TS:AS], valid[b.p][:, TS:AS], 1.0, BIG, ALU.subtract, ALU.mult)
                assert step.count() == STEPS_MEDIUM

            def prepare_dense(b, d):
                step = chain(dve, dense_rank_step, STEPS_RANK * d)
                step(dve.scalar_tensor_tensor(is_dense[:, :], rank[b.p][:, :], P - 0.5, is_long[b.p][:, :],
                                              ALU.is_lt, ALU.subtract))
                step(dve.tensor_scalar(is_dense[:, :], is_dense[:, :], -1.0, None, ALU.mult))
                dve.tensor_copy(dense16[:, :], is_dense[:, :]).then_inc(dense16_ready, 1)
                dve.wait_ge(dense_rank_ps_ready, d + 1)
                step(dve.tensor_copy(rank_sums[:, 0:2 * T], rank_ps[:, 0:2 * T]))
                ranks(step, rank[b.p][:, :], is_dense[:, :])
                assert step.count() == STEPS_RANK

            def long_max(step, q, h):
                n = HEADS * q + h
                dve.wait_ge(scores_ready, n + 1)
                if h >= 2:
                    dve.wait_ge(weights_transposed, 3 * (n - 1))
                alone(dve)
                dve.tensor_tensor_reduce(out=weights[h % 2][:, :],
                                         in0=mid[:, :, :].rearrange("p b n -> p (b n)")[:, 0:N], in1=long_adj[:, :],
                                         scale=1.0, scalar=-3.0e38, op0=ALU.add, op1=ALU.max,
                                         accum_out=row_max[:, h:h + 1]).then_inc(scores_read, 1)
                dve.wait_ge(scores_read, LONG0 + n + 1)
                step(dve.scalar_tensor_tensor(weights[h % 2][:, :], weights[h % 2][:, :], SLOPE, weights[h % 2][:, :],
                                              ALU.mult, ALU.max))
                step(dve.scalar_tensor_tensor(row_lrelu[:, h:h + 1], row_max[:, h:h + 1], SLOPE,
                                              row_max[:, h:h + 1], ALU.mult, ALU.max))
                dve.tensor_scalar(neg_max[:, h:h + 1], row_lrelu[:, h:h + 1], -SCALE, None, ALU.mult
                                  ).then_inc(neg_max_ready, 1)

            def long_copy(q, h):
                n = HEADS * q + h
                for k in range(2):
                    dve.wait_ge(weights_transposed, 3 * n + k + 1)
                    dve.wait_ge(long_out_ready, LONG0 + n)
                    dve.tensor_copy(weightsT[:, 4 * k:4 * k + 4, :],
                                    ring[:, k, :].rearrange("p (c n) -> p c n", c=4)).then_inc(weightsT_by_dve, 1)

            def long_tile(b, q):
                step = chain(dve, long_step, STEPS_LONG * q)
                dve.wait_ge(long_loaded, 32 * (q + 1))
                step(dve.tensor_scalar(long_adj[:, :], long_adj[:, :], 1.0, BIG, ALU.subtract, ALU.mult))
                long_max(step, q, 0)
                for h in range(HEADS):
                    if h + 1 < HEADS:
                        long_max(step, q, h + 1)
                    long_copy(q, h)
                dve.wait_ge(long_out_ready, LONG0 + HEADS * (q + 1))
                step(dve.reciprocal(row_rcp[:, :], row_sum[:, :]))
                la = long_a[:, 0, :]
                step(dve.tensor_tensor(la.rearrange("p (h o) -> p h o", h=HEADS),
                                       long_out.rearrange("p (h o) -> p h o", h=HEADS),
                                       row_rcp[:, :].unsqueeze(2).broadcast_to([P, HEADS, OUT]), ALU.mult))
                step(dve.tensor_tensor(la, la, bias_bc[:, :], ALU.add))
                step(dve.scalar_tensor_tensor(la, la, 0.0, long_x[:, :], ALU.max, ALU.add))
                step(dve.tensor_reduce(long_stat[:, 0:1], la, X, ALU.add))
                step(dve.tensor_scalar(long_stat[:, 0:1], long_stat[:, 0:1], 1.0 / F, None, ALU.mult))
                dve.tensor_scalar(long_b[:, 0, :], la, long_stat[:, 0:1], None, ALU.subtract).then_inc(long_centred, 1)
                dve.wait_ge(long_squared, q + 1)
                step(dve.tensor_reduce(long_stat[:, 1:2], long_sq[:, 0, :], X, ALU.add))
                dve.tensor_scalar(long_stat[:, 1:2], long_stat[:, 1:2], 1.0 / F, EPS, ALU.mult, ALU.add
                                  ).then_inc(long_var, 1)
                dve.wait_ge(long_rstd, q + 1)
                dve.tensor_scalar(long_x1[:, :], long_b[:, 0, :], long_stat[:, 3:4], None, ALU.mult
                                  ).then_inc(long_x1_ready, 1)
                assert step.count() == STEPS_LONG

            def over_features(v, tiles=T):
                return v.unsqueeze(2).broadcast_to([P, tiles, F])

            def layernorm(step, n, tiles):
                step(dve.tensor_reduce(stat[:, 0, 0:tiles], u[:, 0:tiles, :], X, ALU.add))
                step(dve.tensor_scalar(stat[:, 0, 0:tiles], stat[:, 0, 0:tiles], 1.0 / F, None, ALU.mult))
                dve.tensor_tensor(uc[:, 0:tiles, :], u[:, 0:tiles, :], over_features(stat[:, 0, 0:tiles], tiles),
                                  ALU.subtract).then_inc(centred, 1)
                dve.wait_ge(squared, n)
                step(dve.tensor_reduce(stat[:, 1, 0:tiles], sq[:, 0:tiles, :], X, ALU.add))
                dve.tensor_scalar(stat[:, 1, 0:tiles], stat[:, 1, 0:tiles], 1.0 / F, EPS, ALU.mult, ALU.add
                                  ).then_inc(var_ready, 1)
                dve.wait_ge(rstd_ready, n)

            def attend(b):
                step = chain(dve, attend_step, STEPS_ATTEND * b.j)
                dve.wait_ge(y_stored, Y0 + 48 * b.j)
                dve.wait_ge(proj_ready, (T // 2) * (b.j + 1))
                dve.wait_ge(slots_loaded[b.p], 16 * TS * (b.r + 1))
                dve.wait_ge(medium_slots_loaded, 16 * MSLOTS * (b.j + 1))
                dve.wait_ge(medium_rows_loaded, 32 * (b.j + 1))
                G, M = gathered[b.p], medium_gathered
                S, SM = TS * HEADS, AS * HEADS

                def short(v, order="p t s h"):
                    return v[:, 0:S].rearrange("p (t s h) -> " + order, t=T, s=SLOTS)

                def medium(v, order="p s h"):
                    return v[:, S:SM].rearrange("p (s h) -> " + order, h=HEADS)

                def per_tile(v):
                    return v[:, 0:T * HEADS].rearrange("p (t h) -> p t h", t=T)

                dve.tensor_tensor(prod[:, 0:TS * F].rearrange("p (t s f) -> p t s f", t=T, s=SLOTS), G[:, :, :, 0:F],
                                  proj[b.p][:, 0:T, 0:F].unsqueeze(2).broadcast_to([P, T, SLOTS, F]), ALU.mult)
                step(dve.tensor_tensor(prod[:, TS * F:AS * F].rearrange("p (s f) -> p s f", f=F), M[:, :, 0:F],
                                       proj[b.p][:, T, 0:F].unsqueeze(1).broadcast_to([P, MSLOTS, F]), ALU.mult))
                step(dve.tensor_reduce(score[:, :], prod[:, :].rearrange("p (a d) -> p a d", d=ATT), X, ALU.add))
                slot_head = score[:, :].rearrange("p (a h) -> p a h", h=HEADS)
                per_slot = penalty[b.p][:, :].unsqueeze(2).broadcast_to([P, AS, HEADS])
                step(dve.tensor_tensor(slot_head, slot_head, per_slot, ALU.add))
                step(dve.scalar_tensor_tensor(lrelu[:, :], score[:, :], SLOPE, score[:, :], ALU.mult, ALU.max))
                dve.tensor_reduce(per_tile(slot_max), short(lrelu, "p t h s"), X, ALU.max)
                step(dve.tensor_reduce(slot_max[:, T * HEADS:], medium(lrelu, "p h s"), X, ALU.max))
                dve.tensor_tensor(short(score), short(lrelu),
                                  per_tile(slot_max).unsqueeze(2).broadcast_to([P, T, SLOTS, HEADS]), ALU.subtract)
                dve.tensor_tensor(medium(score), medium(lrelu),
                                  slot_max[:, T * HEADS:].unsqueeze(1).broadcast_to([P, MSLOTS, HEADS]), ALU.subtract
                                  ).then_inc(exp_in_ready, 1)
                dve.wait_ge(exp_ready, b.j + 1)
                dve.tensor_reduce(per_tile(den), short(expw, "p t h s"), X, ALU.add)
                step(dve.tensor_reduce(den[:, T * HEADS:], medium(expw, "p h s"), X, ALU.add))
                slot_head = expw[:, :].rearrange("p (a h) -> p a h", h=HEADS)
                per_slot = valid[b.p][:, :].unsqueeze(2).broadcast_to([P, AS, HEADS])
                step(dve.tensor_tensor(slot_head, slot_head, per_slot, ALU.mult))
                by_head = prod[:, :].rearrange("p (a h o) -> p a h o", h=HEADS, o=OUT)
                dve.tensor_tensor(by_head[:, 0:TS], G[:, :, :, F:2 * F].rearrange("p t s (h o) -> p (t s) h o", h=HEADS),
                                  slot_head[:, 0:TS].unsqueeze(3).broadcast_to([P, TS, HEADS, OUT]), ALU.mult)
                dve.tensor_tensor(by_head[:, TS:AS], M[:, :, F:2 * F].rearrange("p s (h o) -> p s h o", h=HEADS),
                                  slot_head[:, TS:AS].unsqueeze(3).broadcast_to([P, MSLOTS, HEADS, OUT]), ALU.mult
                                  ).then_inc(gathered_read, 1)
                dve.wait_ge(gathered_read, ATTEND0 + b.j + 1)
                dve.tensor_reduce(u[:, 0:T, :], prod[:, 0:TS * F].rearrange("p (t s f) -> p t f s", t=T, s=SLOTS),
                                  X, ALU.add)
                step(dve.tensor_reduce(u[:, T, :], prod[:, TS * F:AS * F].rearrange("p (s f) -> p f s", f=F),
                                       X, ALU.add))
                step(dve.reciprocal(den[:, :], den[:, :]))
                flat = u[:, :, :].rearrange("p t (h o) -> p (t h) o", h=HEADS)
                step(dve.tensor_tensor(flat, flat, den[:, :].unsqueeze(2).broadcast_to([P, (T + 1) * HEADS, OUT]),
                                       ALU.mult))
                step(dve.tensor_tensor(u[:, :, :], u[:, :, :], bias_bc[:, :].unsqueeze(1).broadcast_to([P, T + 1, HO]),
                                       ALU.add))
                step(dve.scalar_tensor_tensor(u[:, :, :], u[:, :, :], 0.0, x_in[b.p][:, :, :], ALU.max, ALU.add))
                layernorm(step, 2 * b.j + 1, T + 1)
                dve.tensor_scalar(x1[:, T, :], uc[:, T, :], stat[:, 3, T:T + 1], None, ALU.mult
                                  ).then_inc(medium_x1_ready, 1)
                step(dve.tensor_tensor(x1[:, 0:T, :], uc[:, 0:T, :], over_features(stat[:, 3, 0:T]), ALU.mult))
                assert step.count() == STEPS_ATTEND

            def merge(b):
                dve.wait_ge(merged_loaded[b.p], 16 * (b.r + 1))
                alone(dve)
                dve.copy_predicated(x1[:, 0:T, :], over_features(is_long[b.p][:, :].bitcast(U32)), merged
                                    ).then_inc(part_in_ready, 1)
                dve.wait_ge(part_ready, 2 * b.j + 1)
                dve.tensor_tensor(u[:, 0:T, :], x1[:, 0:T, :], x1_parts[:, :, 0, :], ALU.subtract
                                  ).then_inc(part_in_ready, 1)
                dve.wait_ge(part_ready, 2 * b.j + 2)
                dve.tensor_tensor(x1_parts[:, :, 2, :], u[:, 0:T, :], x1_parts[:, :, 1, :], ALU.subtract
                                  ).then_inc(parts_ready, 1)

            def aggregate(b):
                step = chain(dve, agg_step, STEPS_AGG * b.j)
                messages = prod[:, 0:T * F].rearrange("p (t f) -> p t f", t=T)
                step(dve.tensor_scalar(inv_degree[:, :], degree[b.p][:, :], 1.0, None, ALU.max))
                step(dve.reciprocal(inv_degree[:, :], inv_degree[:, :]))
                for g in range(T // 2):
                    dve.wait_ge(agg_ps_ready, AGG0 + (T // 2) * b.j + g + 1)
                    parts = mid[:, g % 3, :].rearrange("p (t c) -> p t c", t=2)[:, :, 0:3 * F]
                    dve.tensor_reduce(messages[:, 2 * g:2 * g + 2, :], parts.rearrange("p t (a f) -> p t f a", a=3),
                                      X, ALU.add).then_inc(agg_read, 1)
                dve.wait_ge(agg_read, AGG0 + (T // 2) * (b.j + 1))
                step(dve.tensor_tensor(messages, messages, over_features(inv_degree[:, :]), ALU.mult))
                step(dve.tensor_tensor(u[:, 0:T, :], messages, x1[:, 0:T, :], ALU.add))
                layernorm(step, 2 * b.j + 2, T)
                dve.tensor_tensor(y, y, over_features(stat[:, 3, 0:T]), ALU.mult).then_inc(y_ready, 1)
                assert step.count() == STEPS_AGG

            def rest(b, next_b):
                first, end, batches = load_span(dve, b)
                with dve.If(end - first > 0):
                    prepare_dense(b, batches)
                    alone(dve)
                    with dve.Fori(first, end) as q:
                        dve.wait_ge(dense_tile_over, LONG0 + q)
                        make_list(b, dense_list, q + 1, dense_load, dense_store)
                        step = chain(dve, rank_moved, q)
                        step(dve.tensor_scalar(rank[b.p][:, :], rank[b.p][:, :], float(P), None, ALU.subtract))
                        long_tile(b, q)
                attend(b)
                if next_b:
                    extract_medium(next_b)
                merge(b)
                aggregate(b)

            extract(Batch(0, 0, 0))
            extract_medium(Batch(0, 0, 0))
            pipeline(extract, rest, dve)

_INS = ['x', 'adj', 'L0_gnn_kernel', 'L0_gnn_attention_kernel', 'L0_gnn_attention_kernel_2', 'L0_gnn_bias']


def kernel(**inputs):
    import numpy as _np
    import concourse.bacc as _bacc
    from concourse import mybir as _mybir
    from concourse.bass_utils import run_bass_kernel_spmd as _run

    nc = _bacc.Bacc("TRN2", target_bir_lowering=False, num_devices=1)
    arrays, args = {}, []
    for name in _INS:
        a = _np.ascontiguousarray(inputs[name])
        arrays[f"in_{name}_dram"] = a
        args.append(nc.dram_tensor(f"in_{name}_dram", a.shape, _mybir.dt.from_np(a.dtype), kind="ExternalInput").ap())
    args.append(nc.dram_tensor("out_0_dram", inputs["x"].shape, _mybir.dt.float32, kind="ExternalOutput").ap())
    gat_resnorm_kernel(nc, *args)
    r = _run(nc, [arrays], core_ids=[0])
    return r.results[0]["out_0_dram"]
```

```python
from contextlib import ExitStack
from concourse import mybir
import concourse.bass as bass

F32 = mybir.dt.float32
F16 = mybir.dt.float16
BF16 = mybir.dt.bfloat16
F8 = mybir.dt.float8e4
U32 = mybir.dt.uint32
I32 = mybir.dt.int32
ALU = mybir.AluOpType
ACT = mybir.ActivationFunctionType
X = mybir.AxisListType.X

P = 128
HEADS, OUT, ATT = 4, 16, 16
SLOTS = 4
MSLOTS = 11
BIG = 1.0e9
SKIP = 100000.0
SLOPE = 0.2
SCALE = 1.0 / ATT ** 0.5
EPS = 1.0e-5

STEPS_FIRST, STEPS_SPAN, STEPS_EXTRACT, STEPS_LIST, STEPS_MEDIUM, STEPS_RANK, STEPS_LONG, STEPS_ATTEND, STEPS_AGG = (
    2, 9, 13, 2, 6, 7, 17, 17, 7)
LONG_TEST = ALU.not_equal
MEDIUM_DEGREE = MSLOTS


def gat_resnorm_kernel(nc, x, adj, w_feat, w_self, w_other, bias, out):
    B, N, F = x.shape
    T = -(-N // P)
    ROWS = [min(P, N - P * t) for t in range(T)]
    LAST = ROWS[-1]
    LAST16 = LAST // 16 * 16
    HO = HEADS * OUT
    C = HO + 2 * F
    GROUPS = T // 3
    TS = T * SLOTS
    AS = TS + MSLOTS
    assert T % 4 == 0 and T % 3 == 0 and F == HO and B % 2 == 0

    ctx = ExitStack()

    def sb(name, shape, dt=F32):
        return ctx.enter_context(nc.sbuf_tensor(name, shape, dt))

    def ps(name, shape, dt=F32):
        return ctx.enter_context(nc.psum_tensor(name, shape, dt))

    def sem(name):
        return ctx.enter_context(nc.semaphore(name))

    with ctx:
        table = [nc.dram_tensor(f"table{p}", (N, 2 * F), F32, kind="Internal").ap() for p in range(2)]
        self_table = [nc.dram_tensor(f"self_table{p}", (N, F), F32, kind="Internal").ap() for p in range(2)]
        long_x1_dram = [nc.dram_tensor(f"long_x1_{p}", (T * P, F), F32, kind="Internal").ap() for p in range(2)]
        adj_rows = adj.rearrange("b n m -> (b n) m")
        x_rows = x.rearrange("b n f -> (b n) f")

        adj_in = sb("adj_in", [P, 4, N])
        x_in = [sb(f"x_in{p}", [P, T + 1, F]) for p in range(2)]
        proj = [sb(f"proj{p}", [P, T + 1, C]) for p in range(2)]
        adjT = [sb(f"adjT{p}", [P, T, N], F8) for p in range(2)]
        keys = sb("keys", [P, T, 8])
        valid = [sb(f"valid{p}", [P, AS]) for p in range(2)]
        penalty = [sb(f"penalty{p}", [P, AS]) for p in range(2)]
        degree = [sb(f"degree{p}", [P, T]) for p in range(2)]
        is_long = [sb(f"is_long{p}", [P, T]) for p in range(2)]
        index = [sb(f"index{p}", [P, T, SLOTS], U32) for p in range(2)]
        index_skip = sb("index_skip", [P, 3, SLOTS])
        gathered = [sb(f"gathered{p}", [P, T, SLOTS, 2 * F]) for p in range(2)]
        medium_gathered = sb("medium_gathered", [P, MSLOTS, 2 * F])
        medium_keys = sb("medium_keys", [P, 16])
        medium_skip = sb("medium_skip", [P, MSLOTS])
        medium_index = sb("medium_index", [P, MSLOTS], U32)
        node_iota = sb("node_iota", [P, N], F16)
        key_found = sb("key_found", [P, T])
        is_medium = sb("is_medium", [P, T])
        is_dense = sb("is_dense", [P, T])
        total_long = sb("total_long", [P, 1])
        long16 = sb("long16", [P, 2 * T], F16)
        dense16 = sb("dense16", [P, T], F16)
        rank_sums = sb("rank_sums", [P, 3 * T])
        tile_end = sb("tile_end", [P, T])
        rank = [sb(f"rank{p}", [P, T]) for p in range(2)]
        tiles_over = sb("tiles_over", [P, T])
        tiles_used = sb("tiles_used", [P, 1])
        span = sb("span", [P, 4])
        span_int = [sb(f"span_int{p}", [P, 4], I32) for p in range(2)]
        list_vals = sb("list_vals", [P, 2])
        list_skip = sb("list_skip", [P, 1])
        first_row = sb("first_row", [P, 2])
        medium_load = [sb(f"medium_load{p}", [P, 1], U32) for p in range(2)]
        medium_self = [sb(f"medium_self{p}", [P, 1], U32) for p in range(2)]
        medium_store = [sb(f"medium_store{p}", [P, 1], U32) for p in range(2)]
        dense_load = sb("dense_load", [P, 1], U32)
        inv_degree = sb("inv_degree", [P, T])
        dense_store = sb("dense_store", [P, 1], U32)
        long_adj = sb("long_adj", [P, N])
        long_x = sb("long_x", [P, F])
        weights = [sb(f"weights{k}", [P, N]) for k in range(2)]
        xT = weights[0][0:F, :]
        row_max = sb("row_max", [P, HEADS])
        row_lrelu = sb("row_lrelu", [P, HEADS])
        neg_max = sb("neg_max", [P, HEADS])
        row_sum = sb("row_sum", [P, HEADS])
        row_rcp = sb("row_rcp", [P, HEADS])
        long_a = sb("long_a", [P, 1, F])
        long_b = sb("long_b", [P, 1, F])
        long_sq = sb("long_sq", [P, 1, F])
        long_stat = sb("long_stat", [P, 4])
        long_x1 = sb("long_x1", [P, F])
        prod = sb("prod", [P, max(AS * F, TS * F + T * F, T * P // 2 + T * P + N)])
        onehot = prod[:, 0:T * P // 2].bitcast(F16).rearrange("p (t e) -> p t e", t=T)
        weightsT = prod[:, T * P // 2:T * P // 2 + T * P].rearrange("p (t e) -> p t e", t=T)
        otherT = prod[:, T * P // 2 + T * P:T * P // 2 + T * P + N]
        messages = prod[:, TS * F:TS * F + T * F].rearrange("p (t f) -> p t f", t=T)
        merged = prod[:, T * F:2 * T * F].rearrange("p (t f) -> p t f", t=T)
        score = sb("score", [P, AS * HEADS])
        lrelu = sb("lrelu", [P, AS * HEADS])
        slot_max = sb("slot_max", [P, (T + 1) * HEADS])
        expw = score
        den = sb("den", [P, (T + 1) * HEADS])
        u = sb("u", [P, T + 1, F])
        uc = sb("uc", [P, T + 1, F])
        sq = sb("sq", [P, T + 1, F])
        dense_xT = sq[0:F, 0:2, :].rearrange("p t f -> p (t f)")
        dense_selfT = sq[:, 2:4, :].rearrange("p t f -> p (t f)")
        stat = sb("stat", [P, 4, T + 1])
        x1 = sb("x1", [P, T + 1, F])
        x1_parts = sb("x1_parts", [P, T, 3, F], BF16)
        y = uc[:, 0:T, :]
        ident = sb("ident", [P, P])
        w_all = sb("w_all", [F, C])
        w_self_pad = sb("w_self_pad", [F, P])
        w_other_pad = sb("w_other_pad", [F, P])
        bias_bc = sb("bias_bc", [P, HO])
        key_iota = sb("key_iota", [P, T])
        key_mat = sb("key_mat", [P, T, P + 1], F16)
        before = sb("before", [P, P], F16)
        ones = sb("ones", [P, P], F16)
        col_iota = sb("col_iota", [P, P])
        row_names = sb("row_names", [P, T, 2], F16)
        tile_steps = sb("tile_steps", [P, T])
        zero_row = sb("zero_row", [P, T])

        ring = ps("ring", [P, 4, 512])
        mid = ps("mid", [P, 3, 512])
        misc = ps("misc", [P, 512])
        rank_ps = misc[:, 0:3 * T]
        list_ps = misc[:, 48:50]
        long_out = misc[:, 64:64 + HO]
        long_xT_ps = misc[0:F, 128:256]
        long_selfT_ps = misc[:, 256:384]

        weights_in, const_ready, cleared, key_mat_ready, first_contents, psum_cleared = (
            sem("weights_in"), sem("const_ready"), sem("cleared"), sem("key_mat_ready"), sem("first_contents"),
            sem("psum_cleared"))
        scratch_init, pad_ready, mask_ready = sem("scratch_init"), sem("pad_ready"), sem("mask_ready")
        x_loaded = [sem(f"x_loaded{p}") for p in range(2)]
        xT_ps_ready, xT_ready = sem("xT_ps_ready"), sem("xT_ready")
        proj_ps_ready, proj_ready = sem("proj_ps_ready"), sem("proj_ready")
        table_written = [sem(f"table_written{p}") for p in range(2)]
        adj_loaded = [sem(f"adj_loaded{s}") for s in range(4)]
        adj_transposed = sem("adj_transposed")
        adjT_ready = sem("adjT_ready")
        keys_ps_ready, keys_taken, index_ready = sem("keys_ps_ready"), sem("keys_taken"), sem("index_ready")
        message_ready = sem("message_ready")
        first_step, span_step = sem("first_step"), sem("span_step")
        extract_step, long16_ready, rank_ps_ready, span_ready = (
            sem("extract_step"), sem("long16_ready"), sem("rank_ps_ready"), sem("span_ready"))
        medium_list = [sem(f"medium_list_{s}") for s in ("onehot", "ps", "step", "ready")]
        dense_list = [sem(f"dense_list_{s}") for s in ("onehot", "ps", "step", "ready")]
        medium_adj_loaded, medium_rows_loaded, medium_step, medium_index_ready = (
            sem("medium_adj_loaded"), sem("medium_rows_loaded"), sem("medium_step"), sem("medium_index_ready"))
        medium_slots_loaded, medium_x1_ready, medium_stored = (
            sem("medium_slots_loaded"), sem("medium_x1_ready"), sem("medium_stored"))
        dense16_ready, dense_rank_ps_ready, dense_rank_step, rank_moved = (
            sem("dense16_ready"), sem("dense_rank_ps_ready"), sem("dense_rank_step"), sem("rank_moved"))
        dense_xT_ps_ready, dense_xT_ready = sem("dense_xT_ps_ready"), sem("dense_xT_ready")
        otherT_ps_ready, otherT_ready = sem("otherT_ps_ready"), sem("otherT_ready")
        dense_tile_over, dense_over = sem("dense_tile_over"), sem("dense_over")
        slots_loaded = [sem(f"slots_loaded{p}") for p in range(2)]
        short_step = sem("short_step")
        attend_step, exp_in_ready, exp_ready, gathered_read = (
            sem("attend_step"), sem("exp_in_ready"), sem("exp_ready"), sem("gathered_read"))
        centred, squared, var_ready, std_ready = (
            sem("centred"), sem("squared"), sem("var_ready"), sem("std_ready"))
        part_in_ready, part_ready, parts_ready = sem("part_in_ready"), sem("part_ready"), sem("parts_ready")
        long_loaded, long_xT_ps_ready, long_xT_ready = sem("long_loaded"), sem("long_xT_ps_ready"), sem("long_xT_ready")
        selfT_ps_ready, selfT_ready = sem("selfT_ps_ready"), sem("selfT_ready")
        long_step, scores_ready, scores_read, neg_max_ready = (
            sem("long_step"), sem("scores_ready"), sem("scores_read"), sem("neg_max_ready"))
        weights_ready, weights_transposed = sem("weights_ready"), sem("weights_transposed")
        weightsT_by_dve, weightsT_by_act, long_out_ready = (
            sem("weightsT_by_dve"), sem("weightsT_by_act"), sem("long_out_ready"))
        long_centred, long_squared, long_var, long_std = (
            sem("long_centred"), sem("long_squared"), sem("long_var"), sem("long_std"))
        long_x1_ready, long_stored = sem("long_x1_ready"), sem("long_stored")
        merged_loaded = [sem(f"merged_loaded{p}") for p in range(2)]
        agg_ps_ready, agg_read, agg_step, agg_done, y_ready, y_stored = (
            sem("agg_ps_ready"), sem("agg_read"), sem("agg_step"), sem("agg_done"), sem("y_ready"), sem("y_stored"))

        class Batch:

            def __init__(self, j, p, r):
                self.j, self.p, self.r = j, p, r

        AGG0, ATTEND0, LONG0, Y0 = T, 2, 1, 1
        HALVES = ((0, T // 2), (T // 2, T))
        EARLY = 3
        RING0, RING_ACT0 = 12, 4
        starts = ((agg_ps_ready, AGG0), (agg_read, AGG0), (gathered_read, ATTEND0), (parts_ready, ATTEND0),
                  (long_out_ready, LONG0), (scores_read, LONG0), (weightsT_by_act, LONG0), (weightsT_by_dve, LONG0),
                  (dense_tile_over, LONG0), (y_stored, Y0), (adj_transposed, RING0), (adjT_ready, RING_ACT0))
        wait_passed = {e: sem(f"wait_passed_{e}") for e in ("Pool", "Activation", "PE", "DVE", "SP")}

        def alone(eng):
            eng.sem_inc(wait_passed[str(eng.engine).split(".")[-1]], 1)

        def chain(eng, semaphore, base):
            count = [0]

            def step(instruction):
                count[0] += 1
                instruction.then_inc(semaphore, 1)
                eng.wait_ge(semaphore, base + count[0])
            step.count = lambda: count[0]
            return step

        def pipeline(period, eng):
            with eng.Fori(0, B // 2 - 1) as k:
                even, odd = Batch(2 * k, 0, k), Batch(2 * k + 1, 1, k)
                even2, odd2 = Batch(2 * k + 2, 0, k + 1), Batch(2 * k + 3, 1, k + 1)
                period(even, odd, even2)
                period(odd, even2, odd2)
            even, odd = Batch(B - 2, 0, B // 2 - 1), Batch(B - 1, 1, B // 2 - 1)
            period(even, odd, None)
            period(odd, None, None)

        def load_dense_tiles(eng, b):
            eng.wait_ge(span_ready, b.j + 1)
            alone(eng)
            return eng.value_load(span_int[b.p][0:1, 3:4], min_val=0, max_val=T)

        def load_span(eng, b):
            first = eng.value_load(span_int[b.p][0:1, 0:1], min_val=0, max_val=B * T)
            end = eng.value_load(span_int[b.p][0:1, 1:2], min_val=0, max_val=B * T)
            batches = eng.value_load(span_int[b.p][0:1, 2:3], min_val=0, max_val=B)
            return first, end, batches

        def row_dmas(eng, dram, j, tile, store, semaphore):
            for rows, count, t0, t1 in ((0, P, 0, T - 1), (P * (T - 1), LAST16, T - 1, T),
                                        (P * (T - 1) + LAST16, LAST - LAST16, T - 1, T)):
                side = dram[bass.ds(j, 1), rows:rows + (t1 - t0) * count, :].rearrange(
                    "o (t p) f -> p (o t) f", p=count)
                at = rows % P
                part = tile[at:at + count, t0:t1, :]
                src, dst = (part, side) if store else (side, part)
                eng.dma_start(dst, src).then_inc(semaphore, 16)

        block = ctx.enter_context(nc.Block())

        @block.sync
        def _(sp):
            for dst, w in ((w_all[:, 0:F], w_self), (w_all[:, F:2 * F], w_other), (w_all[:, 2 * F:C], w_feat)):
                sp.dma_start(dst.rearrange("f (h o) -> f h o", h=HEADS),
                             w.rearrange("h f o -> f h o")).then_inc(weights_in, 16)
            sp.wait_ge(pad_ready, 3)
            for dst, w in ((w_self_pad, w_self), (w_other_pad, w_other)):
                sp.dma_start(dst[:, :].rearrange("f (h o) -> f h o", h=HEADS)[:, :, 0:ATT],
                             w.rearrange("h f o -> f h o")).then_inc(weights_in, 16)
            sp.dma_start(bias_bc[:, :], bias.rearrange("a b h o -> (a b) (h o)").broadcast_to([P, HO])
                         ).then_inc(weights_in, 16)

            def load_x(b):
                row_dmas(sp, x, b.j, x_in[b.p], False, x_loaded[b.p])

            def load_adj(b, tiles):
                for t in tiles:
                    s = t % 4
                    sp.wait_ge(adj_transposed, RING0 + 3 * (T * b.j + t - 3))
                    for r0, r1 in ((0, P),) if t < T - 1 else ((0, LAST16), (LAST16, LAST)):
                        sp.dma_start(adj_in[r0:r1, s, :], adj[bass.ds(b.j, 1), P * t + r0:P * t + r1, :].rearrange(
                            "o p m -> p (o m)")).then_inc(adj_loaded[s], 16)

            def write_tables(b):
                sp.wait_ge(proj_ready, (T // 2) * (b.j + 1))
                sp.wait_ge(gathered_read, ATTEND0 + b.j - 1)
                for dst, c0, c1 in ((table[b.p], F, C), (self_table[b.p], 0, F)):
                    for r0, r1, t0, t1 in ((0, P, 0, T - 1), (0, LAST16, T - 1, T), (LAST16, LAST, T - 1, T)):
                        row0 = P * t0 + r0
                        rows = dst[row0:row0 + (r1 - r0) * (t1 - t0), :].rearrange("(t p) f -> p t f", p=r1 - r0)
                        sp.dma_start(rows, proj[b.p][r0:r1, t0:t1, c0:c1]).then_inc(table_written[b.p], 16)

            def read_back(b):
                sp.wait_ge(medium_stored, 16 * (b.j + 1))
                sp.wait_ge(dense_over, b.j + 1)
                sp.dma_start(merged[:, :, :], long_x1_dram[b.p].rearrange("(t p) f -> p t f", p=P)
                             ).then_inc(merged_loaded[b.p], 16)

            def store_y(b):
                sp.wait_ge(y_ready, b.j + 1)
                row_dmas(sp, out, b.j, y, True, y_stored)

            def period(b, next_b, after_next):
                if next_b:
                    load_adj(next_b, range(4 + EARLY, T))
                if after_next:
                    load_adj(after_next, range(4))
                    sp.wait_ge(centred, 2 * b.j + 1)
                    load_x(after_next)
                read_back(b)
                if after_next:
                    write_tables(after_next)
                    load_adj(after_next, range(4, 4 + EARLY))
                store_y(b)

            batch0, batch1 = Batch(0, 0, 0), Batch(1, 1, 0)
            load_x(batch0)
            sp.wait_ge(cleared, 1)
            for p in range(2):
                sp.dma_start(long_x1_dram[p].rearrange("(p a) f -> p (a f)", p=P),
                             sq[:, 0:T, :].rearrange("p t f -> p (t f)")).then_inc(scratch_init, 16)
            load_adj(batch0, range(4))
            load_x(batch1)
            write_tables(batch0)
            load_adj(batch0, range(4, T))
            load_adj(batch1, range(4))
            write_tables(batch1)
            load_adj(batch1, range(4, 4 + EARLY))
            pipeline(period, sp)
            sp.wait_ge(y_stored, Y0 + 48 * B)

        @block.gpsimd
        def _(pool):
            for semaphore, count in starts:
                pool.sem_inc(semaphore, count)
            pool.memset(w_self_pad[:, :], 0.0)
            pool.memset(w_other_pad[:, :], 0.0).then_inc(pad_ready, 1)
            for p in range(2):
                pool.memset(x_in[p][:, T - 1, :], 0.0).then_inc(pad_ready, 1)
            pool.memset(sq[:, :, :], 0.0).then_inc(cleared, 1)
            pool.memset(ident[:, :], 0.0).then_inc(mask_ready, 1)
            pool.memset(before[:, :], 1.0).then_inc(mask_ready, 1)
            pool.memset(ones[:, :], 1.0).then_inc(const_ready, 1)
            pool.memset(row_names[:, :, 1:2], 1.0).then_inc(const_ready, 1)
            pool.iota(key_iota[:, :], pattern=[[P, T]], base=1, channel_multiplier=1,
                      allow_small_or_imprecise_dtypes=True).then_inc(const_ready, 1)
            pool.iota(col_iota[:, :], pattern=[[1, P]], base=0, channel_multiplier=0,
                      allow_small_or_imprecise_dtypes=True).then_inc(const_ready, 1)
            pool.iota(row_names[:, :, 0:1], pattern=[[P, T]], base=0, channel_multiplier=1,
                      allow_small_or_imprecise_dtypes=True).then_inc(const_ready, 1)
            pool.iota(tile_steps[:, :], pattern=[[P, T]], base=0, channel_multiplier=0,
                      allow_small_or_imprecise_dtypes=True).then_inc(const_ready, 1)
            pool.iota(node_iota[:, :], pattern=[[1, N]], base=1, channel_multiplier=0,
                      allow_small_or_imprecise_dtypes=True).then_inc(const_ready, 1)
            pool.wait_ge(mask_ready, 2)
            pool.affine_select(out=ident[:, :], in_=ident[:, :], compare_op=ALU.not_equal, fill=1.0,
                               base=0, pattern=[[-1, P]], channel_multiplier=1).then_inc(const_ready, 1)
            pool.affine_select(out=before[:, :], in_=before[:, :], compare_op=ALU.is_gt, fill=0.0,
                               base=0, pattern=[[1, P]], channel_multiplier=-1).then_inc(const_ready, 1)
            pool.memset(gathered[0][:, :, :, :], 0.0).then_inc(cleared, 1)
            pool.memset(gathered[1][:, :, :, :], 0.0).then_inc(cleared, 1)
            pool.memset(medium_gathered[:, :, :], 0.0).then_inc(cleared, 1)

            def gather_slots(b, tiles):
                if tiles[0] == 0:
                    pool.wait_ge(table_written[b.p], 96 * (b.r + 1))
                    pool.wait_ge(gathered_read, ATTEND0 + b.j - 1)
                for t in tiles:
                    if t % 3 == 0:
                        pool.wait_ge(index_ready, GROUPS * b.j + t // 3 + 1)
                        alone(pool)
                    for s in range(SLOTS):
                        pool.indirect_dma_start(
                            gathered[b.p][0:ROWS[t], t, s, :], None, table[b.p],
                            bass.IndirectOffsetOnAxis(ap=index[b.p][0:ROWS[t], t, s:s + 1], axis=0),
                            bounds_check=N - 1, oob_is_err=False).then_inc(slots_loaded[b.p], 16)

            def gather(dst, src, index, rows, semaphore):
                pool.indirect_dma_start(dst, None, src, bass.IndirectOffsetOnAxis(ap=index, axis=0),
                                        bounds_check=rows - 1, oob_is_err=False).then_inc(semaphore, 16)

            def scatter(b, src, index, semaphore):
                pool.indirect_dma_start(long_x1_dram[b.p], bass.IndirectOffsetOnAxis(ap=index, axis=0), src, None,
                                        bounds_check=T * P - 1, oob_is_err=False).then_inc(semaphore, 16)

            def load_medium_adj(b):
                pool.wait_ge(medium_list[3], b.j + 1)
                alone(pool)
                gather(long_adj[:, :], adj_rows, medium_load[b.p][:, 0:1], B * N, medium_adj_loaded)

            def load_medium_rows(b):
                gather(x_in[b.p][:, T, :], x_rows, medium_load[b.p][:, 0:1], B * N, medium_rows_loaded)
                gather(proj[b.p][:, T, 0:F], self_table[b.p], medium_self[b.p][:, 0:1], N, medium_rows_loaded)

            def gather_medium_slots(b):
                pool.wait_ge(medium_index_ready, b.j + 1)
                pool.wait_ge(gathered_read, ATTEND0 + b.j)
                alone(pool)
                for s in range(MSLOTS):
                    gather(medium_gathered[:, s, :], table[b.p], medium_index[:, s:s + 1], N, medium_slots_loaded)

            def store_medium(b):
                pool.wait_ge(medium_x1_ready, b.j + 1)
                alone(pool)
                scatter(b, x1[:, T, :], medium_store[b.p][:, 0:1], medium_stored)

            def dense(b):
                with pool.If(load_dense_tiles(pool, b) > 0):
                    first, end, _ = load_span(pool, b)
                    with pool.Fori(first, end) as q:
                        pool.wait_ge(dense_list[3], q + 1)
                        alone(pool)
                        gather(long_adj[:, :], adj_rows, dense_load[:, 0:1], B * N, long_loaded)
                        gather(long_x[:, :], x_rows, dense_load[:, 0:1], B * N, long_loaded)
                        pool.wait_ge(long_x1_ready, q + 1)
                        alone(pool)
                        scatter(b, long_x1[:, :], dense_store[:, 0:1], long_stored)
                        pool.wait_ge(long_stored, 16 * (q + 1))
                        pool.sem_inc(dense_tile_over, 1)
                pool.sem_inc(dense_over, 1)

            def next_batch(b, done):
                dense(done)
                gather_slots(b, range(0, T - 4))
                load_medium_adj(b)
                store_medium(done)
                load_medium_rows(b)
                gather_slots(b, range(T - 4, T))
                gather_medium_slots(b)

            batch0 = Batch(0, 0, 0)
            pool.wait_ge(scratch_init, 32)
            pool.wait_ge(cleared, 4)
            gather_slots(batch0, range(0, T // 2))
            load_medium_adj(batch0)
            load_medium_rows(batch0)
            gather_slots(batch0, range(T // 2, T))
            gather_medium_slots(batch0)
            with pool.Fori(0, B // 2 - 1) as k:
                next_batch(Batch(2 * k + 1, 1, k), Batch(2 * k, 0, k))
                next_batch(Batch(2 * k + 2, 0, k + 1), Batch(2 * k + 1, 1, k))
            next_batch(Batch(B - 1, 1, B // 2 - 1), Batch(B - 2, 0, B // 2 - 1))
            last = Batch(B - 1, 1, B // 2 - 1)
            dense(last)
            store_medium(last)

        @block.tensor
        def _(pe):
            pe.wait_ge(weights_in, 16 * 6)
            pe.wait_ge(const_ready, 9)
            pe.wait_ge(key_mat_ready, 1)
            pe.wait_ge(psum_cleared, 1)

            def project(b):
                pe.wait_ge(x_loaded[b.p], 48 * (b.r + 1))
                alone(pe)
                for t in range(T):
                    last = pe.transpose(mid[0:F, t // 4, P * (t % 4):P * (t % 4) + ROWS[t]],
                                        x_in[b.p][0:ROWS[t], t, :], ident[0:ROWS[t], 0:ROWS[t]])
                    if t % 4 == 3:
                        last.then_inc(xT_ps_ready, 1)
                for g in range(T // 2):
                    if g < 3:
                        pe.wait_ge(xT_ready, 3 * b.j + g + 1)
                    else:
                        pe.wait_ge(proj_ready, (T // 2) * b.j + g - 2)
                    for t in (2 * g, 2 * g + 1):
                        pe.wait_ge(xT_ready, 3 * b.j + t // 4 + 1)
                        last = pe.matmul(mid[0:ROWS[t], g % 3, 256 * (t % 2):256 * (t % 2) + C],
                                         xT[:, P * t:P * t + ROWS[t]], w_all[:, :], start=True, stop=True)
                    last.then_inc(proj_ps_ready, 1)

            def transpose_tile(b, t):
                s = t % 4
                more = 16 if t == T - 1 else 0
                loads = 64 if s == 3 else 48
                pe.wait_ge(adj_loaded[s], loads * b.j + 16 * (t // 4 + 1) + more)
                for k in range(3):
                    pe.wait_ge(adjT_ready, RING_ACT0 + 3 * (T * b.j + t) + k - 3)
                    for c in range(4 * k, 4 * k + 4):
                        last = pe.transpose(ring[0:ROWS[c], (3 * t + k) % 4, P * (c % 4):P * (c % 4) + ROWS[t]],
                                            adj_in[0:ROWS[t], s, P * c:P * c + ROWS[c]],
                                            ident[0:ROWS[t], 0:ROWS[t]])
                    last.then_inc(adj_transposed, 1)

            def keys_of_tile(b, t):
                g = t // 3
                if t % 3 == 0:
                    if g < 3:
                        pe.wait_ge(proj_ready, (T // 2) * b.j + 3 + g + 1)
                        pe.wait_ge(agg_read, AGG0 + (T // 2) * (b.j - 2) + 3 + g + 1)
                    else:
                        pe.wait_ge(keys_taken, GROUPS * b.j + g - 2)
                pe.wait_ge(adjT_ready, RING_ACT0 + 3 * (T * b.j + t + 1))
                alone(pe)
                for c in range(T):
                    last = pe.matmul(mid[0:ROWS[t], g % 3, (P + 1) * (t % 3):(P + 1) * (t % 3 + 1)],
                                     adjT[b.p][0:ROWS[c], c, P * t:P * t + ROWS[t]],
                                     key_mat[0:ROWS[c], c, :], start=(c == 0), stop=(c == T - 1))
                if t % 3 == 2:
                    last.then_inc(keys_ps_ready, 1)

            def list_rows(sems, count):
                pe.wait_ge(sems[0], count)
                for t in range(T):
                    last = pe.matmul(list_ps, onehot[:, t, :], row_names[:, t, :],
                                     start=(t == 0), stop=(t == T - 1))
                last.then_inc(sems[1], 1)

            def extract(b, tiles):
                for t in tiles:
                    transpose_tile(b, t)
                    if t > tiles[0]:
                        keys_of_tile(b, t - 1)
                keys_of_tile(b, tiles[-1])

            def list_medium(b):
                pe.wait_ge(long16_ready, b.j + 1)
                pe.matmul(rank_ps[:, 0:T], before[:, :], long16[:, 0:T], start=True, stop=True)
                pe.matmul(rank_ps[:, T:3 * T], ones[:, :], long16[:, :], start=True, stop=True
                          ).then_inc(rank_ps_ready, 1)
                list_rows(medium_list, b.j + 1)

            def long_scores(b, q, h):
                pe.wait_ge(scores_read, LONG0 + HEADS * q + h)
                for c in range(3):
                    cols = min(512, N - 512 * c)
                    last = pe.matmul(mid[:, c, 0:cols], dense_selfT[32 * h:32 * h + ATT, :],
                                     otherT[32 * h:32 * h + ATT, 512 * c:512 * c + cols],
                                     start=True, stop=True)
                last.then_inc(scores_ready, 1)

            def long_transposes(q, h):
                pe.wait_ge(weights_ready, HEADS * q + h + 1)
                for k in range(3):
                    if k < 2:
                        pe.wait_ge(weightsT_by_dve, LONG0 + 2 * (HEADS * q + h))
                    else:
                        pe.wait_ge(weightsT_by_act, LONG0 + HEADS * q + h)
                    for c in range(4 * k, 4 * k + 4):
                        last = pe.transpose(ring[0:ROWS[c], k, P * (c % 4):P * (c % 4) + P],
                                            weights[h % 2][:, P * c:P * c + ROWS[c]], ident[:, :])
                    last.then_inc(weights_transposed, 1)

            def long_products(b, q, h):
                pe.wait_ge(weightsT_by_dve, LONG0 + 2 * (HEADS * q + h + 1))
                pe.wait_ge(weightsT_by_act, LONG0 + HEADS * q + h + 1)
                for c in range(T):
                    last = pe.matmul(long_out[:, OUT * h:OUT * (h + 1)], weightsT[0:ROWS[c], c, :],
                                     proj[b.p][0:ROWS[c], c, 2 * F + OUT * h:2 * F + OUT * (h + 1)],
                                     start=(c == 0), stop=(c == T - 1))
                last.then_inc(long_out_ready, 1)

            def long_tile(b, q):
                pe.wait_ge(long_loaded, 32 * (q + 1))
                alone(pe)
                pe.transpose(long_xT_ps, long_x[:, :], ident[:, :]).then_inc(long_xT_ps_ready, 1)
                pe.wait_ge(long_xT_ready, q + 1)
                pe.matmul(long_selfT_ps, w_self_pad[:, :], dense_xT[:, :], start=True, stop=True
                          ).then_inc(selfT_ps_ready, 1)
                pe.wait_ge(selfT_ready, q + 1)
                long_scores(b, q, 0)
                for h in range(HEADS):
                    if h + 1 < HEADS:
                        long_scores(b, q, h + 1)
                    long_transposes(q, h)
                    long_products(b, q, h)

            def prepare_dense(b, d):
                pe.wait_ge(dense16_ready, d + 1)
                pe.matmul(rank_ps[:, 0:T], before[:, :], dense16[:, :], start=True, stop=True)
                pe.matmul(rank_ps[:, T:2 * T], ones[:, :], dense16[:, :], start=True, stop=True
                          ).then_inc(dense_rank_ps_ready, 1)
                for t in range(T):
                    last = pe.transpose(mid[0:F, t // 4, P * (t % 4):P * (t % 4) + ROWS[t]],
                                        x_in[b.p][0:ROWS[t], t, :], ident[0:ROWS[t], 0:ROWS[t]])
                    if t % 4 == 3:
                        last.then_inc(dense_xT_ps_ready, 1)
                for c in range(3):
                    pe.wait_ge(dense_xT_ready, 3 * d + c + 1)
                    cols = min(512, N - 512 * c)
                    pe.matmul(mid[:, c, 0:cols], w_other_pad[:, :], xT[:, 512 * c:512 * c + cols],
                              start=True, stop=True).then_inc(otherT_ps_ready, 1)
                pe.wait_ge(otherT_ready, 3 * d + 3)

            def dense(b, next_b):
                pe.wait_ge(medium_list[3], b.j + 1)
                with pe.If(load_dense_tiles(pe, b) > 0):
                    first, end, batches = load_span(pe, b)
                    pe.wait_ge(adjT_ready, RING_ACT0 + 3 * (T * (b.j + 1) + (EARLY if next_b else 0)))
                    pe.wait_ge(keys_taken, GROUPS * (b.j + 1) + (1 if next_b else 0))
                    pe.wait_ge(agg_read, AGG0 + (T // 2) * b.j)
                    alone(pe)
                    prepare_dense(b, batches)
                    alone(pe)
                    with pe.Fori(first, end) as q:
                        list_rows(dense_list, q + 1)
                        pe.wait_ge(dense_list[3], q + 1)
                        long_tile(b, q)
                    pe.wait_ge(weightsT_by_dve, LONG0 + 2 * HEADS * end)
                    pe.wait_ge(weightsT_by_act, LONG0 + HEADS * end)
                    pe.wait_ge(scores_read, LONG0 + HEADS * end)
                    alone(pe)

            def aggregate(b, projected):
                if projected:
                    pe.wait_ge(proj_ready, (T // 2) * (projected.j + 1))
                for t in range(T):
                    g = t // 2
                    if t % 2 == 0 and g >= 3:
                        pe.wait_ge(agg_read, AGG0 + (T // 2) * b.j + g - 2)
                    if t % 2 == 0 and (g == 0 or g >= 3):
                        alone(pe)
                    for c in range(T):
                        if t == 0 and c in (0, T // 2):
                            pe.wait_ge(parts_ready, ATTEND0 + 2 * b.j + (1 if c == 0 else 2))
                            alone(pe)
                        last = pe.matmul(mid[0:ROWS[t], g % 3, 256 * (t % 2):256 * (t % 2) + 3 * F],
                                         adjT[b.p][0:ROWS[c], c, P * t:P * t + ROWS[t]],
                                         x1_parts[0:ROWS[c], c, :, :].rearrange("p a f -> p (a f)"),
                                         start=(c == 0), stop=(c == T - 1))
                    if t % 2 == 1:
                        last.then_inc(agg_ps_ready, 1)

            def period(b, next_b, after_next):
                dense(b, next_b)
                if next_b:
                    extract(next_b, range(EARLY, T))
                    list_medium(next_b)
                if after_next:
                    project(after_next)
                aggregate(b, after_next)
                if after_next:
                    extract(after_next, range(EARLY))

            batch0, batch1 = Batch(0, 0, 0), Batch(1, 1, 0)
            project(batch0)
            extract(batch0, range(T))
            list_medium(batch0)
            project(batch1)
            extract(batch1, range(EARLY))
            pipeline(period, pe)

        @block.scalar
        def _(act):
            act.wait_ge(scratch_init, 32)

            def copy_xT(b):
                for u3 in range(3):
                    act.wait_ge(xT_ps_ready, 3 * b.j + u3 + 1)
                    cols = min(512, N - 512 * u3)
                    act.copy(xT[:, 512 * u3:512 * u3 + cols], mid[0:F, u3, 0:cols]).then_inc(xT_ready, 1)

            def copy_proj(b, groups):
                act.wait_ge(gathered_read, ATTEND0 + b.j - 1)
                for g in groups:
                    act.wait_ge(proj_ps_ready, (T // 2) * b.j + g + 1)
                    act.copy(proj[b.p][:, 2 * g:2 * g + 2, :],
                             mid[:, g % 3, :].rearrange("p (t c) -> p t c", t=2)[:, :, 0:C]
                             ).then_inc(proj_ready, 1)

            def copy_adjT(b, tiles):
                act.wait_ge(agg_ps_ready, AGG0 + (T // 2) * (b.j - 1))
                for t in tiles:
                    for k in range(3):
                        act.wait_ge(adj_transposed, RING0 + 3 * (T * b.j + t) + k + 1)
                        alone(act)
                        act.copy(adjT[b.p][:, 4 * k:4 * k + 4, P * t:P * t + ROWS[t]],
                                 ring[:, (3 * t + k) % 4, :].rearrange("p (c n) -> p c n", c=4)[:, :, 0:ROWS[t]],
                                 saturate=False).then_inc(adjT_ready, 1)

            def long_tile(b, q):
                act.wait_ge(long_xT_ps_ready, q + 1)
                act.copy(dense_xT[:, :], long_xT_ps).then_inc(long_xT_ready, 1)
                act.wait_ge(selfT_ps_ready, q + 1)
                act.copy(dense_selfT[:, :], long_selfT_ps).then_inc(selfT_ready, 1)
                for h in range(HEADS):
                    n = HEADS * q + h
                    act.wait_ge(neg_max_ready, n + 1)
                    act.activation(weights[h % 2][:, :], weights[h % 2][:, :], ACT.Exp,
                                   bias=neg_max[:, h:h + 1], scale=SCALE,
                                   accum_out=row_sum[:, h:h + 1]).then_inc(weights_ready, 1)
                    act.wait_ge(weights_transposed, 3 * n + 3)
                    act.wait_ge(long_out_ready, LONG0 + n)
                    act.copy(weightsT[:, 8:12, :], ring[:, 2, :].rearrange("p (c n) -> p c n", c=4)
                             ).then_inc(weightsT_by_act, 1)
                act.wait_ge(long_centred, q + 1)
                act.activation(long_sq[:, :, :], long_b[:, :, :], ACT.Square).then_inc(long_squared, 1)
                act.wait_ge(long_var, q + 1)
                act.activation(long_stat[:, 2:3], long_stat[:, 1:2], ACT.Sqrt).then_inc(long_std, 1)

            def squares(n, t0, t1):
                act.wait_ge(centred, n)
                act.activation(sq[:, t0:t1, :], uc[:, t0:t1, :], ACT.Square).then_inc(squared, 1)

            def root(n, t0, t1):
                act.wait_ge(var_ready, n)
                act.activation(stat[:, 2, t0:t1], stat[:, 1, t0:t1], ACT.Sqrt).then_inc(std_ready, 1)

            def prepare_dense(d):
                for c in range(3):
                    act.wait_ge(dense_xT_ps_ready, 3 * d + c + 1)
                    cols = min(512, N - 512 * c)
                    act.copy(xT[:, 512 * c:512 * c + cols], mid[0:F, c, 0:cols]).then_inc(dense_xT_ready, 1)
                for c in range(3):
                    act.wait_ge(otherT_ps_ready, 3 * d + c + 1)
                    cols = min(512, N - 512 * c)
                    act.copy(otherT[:, 512 * c:512 * c + cols], mid[:, c, 0:cols]).then_inc(otherT_ready, 1)

            def dense(b):
                with act.If(load_dense_tiles(act, b) > 0):
                    first, end, batches = load_span(act, b)
                    prepare_dense(batches)
                    with act.Fori(first, end) as q:
                        long_tile(b, q)

            def period(b, next_b, after_next):
                dense(b)
                if next_b:
                    copy_adjT(next_b, range(EARLY, EARLY + 2))
                act.wait_ge(exp_in_ready, b.j + 1)
                act.activation(score[:, :], score[:, :], ACT.Exp, scale=SCALE).then_inc(exp_ready, 1)
                if next_b:
                    copy_adjT(next_b, range(EARLY + 2, T))
                squares(2 * b.j + 1, 0, T + 1)
                root(2 * b.j + 1, 0, T + 1)
                if after_next:
                    copy_xT(after_next)
                    copy_proj(after_next, range(T // 2))
                act.wait_ge(agg_ps_ready, AGG0 + (T // 2) * b.j)
                for part, rest in ((0, x1), (1, u)):
                    for i, (t0, t1) in enumerate(HALVES):
                        act.wait_ge(part_in_ready, 4 * b.j + 2 * part + i + 1)
                        act.copy(x1_parts[:, t0:t1, part, :], rest[:, t0:t1, :]).then_inc(part_ready, 1)
                for t in range(T):
                    act.wait_ge(agg_read, AGG0 + (T // 2) * b.j + t // 2 + 1)
                    act.activation(messages[:, t, :], messages[:, t, :], ACT.Identity, scale=inv_degree[:, t:t + 1]
                                   ).then_inc(message_ready, 1)
                if after_next:
                    copy_adjT(after_next, range(EARLY))
                squares(2 * b.j + 2, 0, T)
                root(2 * b.j + 2, 0, T)

            for b, tiles in ((Batch(0, 0, 0), T), (Batch(1, 1, 0), EARLY)):
                copy_xT(b)
                copy_proj(b, range(T // 2))
                copy_adjT(b, range(tiles))
            pipeline(period, act)

        @block.vector
        def _(dve):
            dve.memset(ring[:, :, :], 0.0)
            dve.memset(mid[:, :, :], 0.0)
            dve.memset(misc[:, :], 0.0).then_inc(psum_cleared, 1)
            for p in range(2):
                dve.memset(degree[p][:, :], 0.0)
                dve.memset(first_row[:, p:p + 1], float(N * (p - 2)))
            dve.memset(keys[:, :, :], 0.0)
            dve.memset(zero_row[:, :], 0.0)
            dve.memset(span[:, :], 0.0)
            dve.memset(tiles_over[:, :], 0.0)
            dve.memset(key_mat[:, :, P:P + 1], 1.0).then_inc(first_contents, 1)
            dve.wait_ge(first_contents, 1)
            dve.wait_ge(const_ready, 9)
            dve.tensor_tensor(key_mat[:, :, 0:P], ident[:, :].unsqueeze(1).broadcast_to([P, T, P]),
                              key_iota[:, :].unsqueeze(2).broadcast_to([P, T, P]), ALU.mult
                              ).then_inc(key_mat_ready, 1)
            dve.wait_ge(key_mat_ready, 1)
            dve.wait_ge(weights_in, 16 * 6)

            def make_onehot(b, sems):
                dve.tensor_tensor(onehot[:, :, :], rank[b.p][:, :].unsqueeze(2).broadcast_to([P, T, P]),
                                  col_iota[:, :].unsqueeze(1).broadcast_to([P, T, P]), ALU.is_equal
                                  ).then_inc(sems[0], 1)

            def read_list(b, sems, count, load, store, row=None):
                _, ps_sem, step_sem, ready_sem = sems
                step = chain(dve, step_sem, STEPS_LIST * (count - 1))
                dve.wait_ge(ps_sem, count)
                step(dve.tensor_copy(list_vals[:, :], list_ps))
                dve.tensor_scalar(load[:, :], list_vals[:, 0:1], first_row[:, b.p:b.p + 1], None, ALU.add)
                if row is not None:
                    dve.tensor_copy(row[:, :], list_vals[:, 0:1])
                step(dve.tensor_scalar(list_skip[:, :], list_vals[:, 1:2], -SKIP, SKIP, ALU.mult, ALU.add))
                dve.tensor_tensor(store[:, :], list_vals[:, 0:1], list_skip[:, :], ALU.add
                                  ).then_inc(ready_sem, 1)
                assert step.count() == STEPS_LIST

            def take_keys(b, g, step):
                dve.wait_ge(keys_ps_ready, GROUPS * b.j + g + 1)
                alone(dve)
                for t in range(3 * g, 3 * g + 3):
                    at = (P + 1) * (t % 3)
                    dve.max(keys[0:ROWS[t], t, :], mid[0:ROWS[t], g % 3, at:at + P])
                counts = mid[:, g % 3, 0:3 * (P + 1)].rearrange("p (t c) -> p t c", t=3)[:, :, P]
                if g == GROUPS - 1:
                    dve.tensor_copy(degree[b.p][0:LAST, T - 1:T], counts[0:LAST, 2:3])
                    dve.tensor_copy(degree[b.p][:, 3 * g:T - 1], counts[:, 0:2]).then_inc(keys_taken, 1)
                else:
                    dve.tensor_copy(degree[b.p][:, 3 * g:3 * g + 3], counts).then_inc(keys_taken, 1)
                dve.wait_ge(keys_taken, GROUPS * b.j + g + 1)
                found = keys[:, 3 * g:3 * g + 3, 0:SLOTS]
                step(dve.tensor_scalar(index_skip[:, :, :], found, 0.5, SKIP, ALU.is_lt, ALU.mult))
                dve.scalar_tensor_tensor(index[b.p][:, 3 * g:3 * g + 3, :], found, -1.0, index_skip[:, :, :],
                                         ALU.add, ALU.add).then_inc(index_ready, 1)

            def ranks(step, r, member):
                step(dve.tensor_tensor_scan(tile_end[:, :], rank_sums[:, T:2 * T], zero_row[:, :], 0.0,
                                            ALU.add, ALU.add))
                step(dve.scalar_tensor_tensor(r, member, -1.0e4, rank_sums[:, 0:T], ALU.mult, ALU.add))
                step(dve.scalar_tensor_tensor(r, r, 1.0e4, tile_end[:, :], ALU.add, ALU.add))
                step(dve.tensor_tensor(r, r, rank_sums[:, T:2 * T], ALU.subtract))

            def kinds(b, step):
                slots = valid[b.p][:, 0:TS].rearrange("p (t s) -> p t s", t=T)
                step(dve.tensor_scalar(slots, keys[:, :, 0:SLOTS], 0.5, None, ALU.is_gt))
                dve.tensor_scalar(penalty[b.p][:, 0:TS], valid[b.p][:, 0:TS], 1.0, BIG, ALU.subtract, ALU.mult)
                step(dve.tensor_reduce(key_found[:, :], slots, X, ALU.add))
                step(dve.tensor_tensor(is_long[b.p][:, :], key_found[:, :], degree[b.p][:, :], LONG_TEST))
                step(dve.scalar_tensor_tensor(is_medium[:, :], degree[b.p][:, :], MEDIUM_DEGREE + 0.5, is_long[b.p][:, :],
                                              ALU.is_lt, ALU.mult))
                step(dve.tensor_copy(long16[:, T:2 * T], is_long[b.p][:, :]))
                dve.tensor_copy(long16[:, 0:T], is_medium[:, :]).then_inc(long16_ready, 1)

            def medium_ranks(b, step):
                dve.wait_ge(rank_ps_ready, b.j + 1)
                step(dve.tensor_copy(rank_sums[:, :], rank_ps))
                ranks(step, rank[b.p][:, :], is_medium[:, :])
                make_onehot(b, medium_list)

            def dense_tiles(b):
                step = chain(dve, span_step, STEPS_SPAN * b.j)
                step(dve.tensor_reduce(total_long[:, :], rank_sums[:, 2 * T:3 * T], X, ALU.add))
                step(dve.scalar_tensor_tensor(total_long[:, :], tile_end[:, T - 1:T], float(P), total_long[:, :],
                                              ALU.min, ALU.subtract))
                step(dve.tensor_scalar(total_long[:, :], total_long[:, :], -1.0, None, ALU.mult))
                step(dve.tensor_tensor(span[:, 2:3], span[:, 2:3], tiles_over[:, 0:1], ALU.add))
                step(dve.tensor_scalar(tiles_over[:, :], tile_steps[:, :], total_long[:, :], None, ALU.is_lt))
                step(dve.tensor_reduce(tiles_used[:, :], tiles_over[:, :], X, ALU.add))
                step(dve.tensor_copy(span[:, 0:1], span[:, 1:2]))
                step(dve.tensor_tensor(span[:, 1:2], span[:, 1:2], tiles_used[:, :], ALU.add))
                step(dve.tensor_copy(span[:, 3:4], tiles_used[:, :]))
                dve.tensor_copy(span_int[b.p][:, :], span[:, :]).then_inc(span_ready, 1)
                assert step.count() == STEPS_SPAN

            def medium_rows(b):
                read_list(b, medium_list, b.j + 1, medium_load[b.p], medium_store[b.p], medium_self[b.p])

            def extract_medium(b, step):
                dve.wait_ge(medium_adj_loaded, 16 * (b.j + 1))
                step(dve.tensor_tensor(long_adj[:, :], long_adj[:, :], node_iota[:, :], ALU.mult))
                alone(dve)
                step(dve.max(medium_keys[:, 0:8], long_adj[:, :]))

            def extract_more(b, step):
                alone(dve)
                step(dve.match_replace(long_adj[:, :], medium_keys[:, 0:8], long_adj[:, :], 0.0))
                alone(dve)
                step(dve.max(medium_keys[:, 8:16], long_adj[:, :]))
                found = medium_keys[:, 0:MSLOTS]
                step(dve.tensor_scalar(medium_skip[:, :], found, 0.5, SKIP, ALU.is_lt, ALU.mult))
                dve.scalar_tensor_tensor(medium_index[:, :], found, -1.0, medium_skip[:, :], ALU.add, ALU.add
                                         ).then_inc(medium_index_ready, 1)
                step(dve.tensor_scalar(valid[b.p][:, TS:AS], found, 0.5, None, ALU.is_gt))
                dve.tensor_scalar(penalty[b.p][:, TS:AS], valid[b.p][:, TS:AS], 1.0, BIG, ALU.subtract, ALU.mult)
                assert step.count() == STEPS_MEDIUM

            def prepare_dense(b, d):
                step = chain(dve, dense_rank_step, STEPS_RANK * d)
                step(dve.scalar_tensor_tensor(is_dense[:, :], rank[b.p][:, :], P - 0.5, is_long[b.p][:, :],
                                              ALU.is_lt, ALU.subtract))
                step(dve.tensor_scalar(is_dense[:, :], is_dense[:, :], -1.0, None, ALU.mult))
                dve.tensor_copy(dense16[:, :], is_dense[:, :]).then_inc(dense16_ready, 1)
                dve.wait_ge(dense_rank_ps_ready, d + 1)
                step(dve.tensor_copy(rank_sums[:, 0:2 * T], rank_ps[:, 0:2 * T]))
                ranks(step, rank[b.p][:, :], is_dense[:, :])
                assert step.count() == STEPS_RANK

            def long_max(step, q, h):
                n = HEADS * q + h
                dve.wait_ge(scores_ready, n + 1)
                if h >= 2:
                    dve.wait_ge(weights_transposed, 3 * (n - 1))
                alone(dve)
                dve.tensor_tensor_reduce(out=weights[h % 2][:, :],
                                         in0=mid[:, :, :].rearrange("p b n -> p (b n)")[:, 0:N], in1=long_adj[:, :],
                                         scale=1.0, scalar=-3.0e38, op0=ALU.add, op1=ALU.max,
                                         accum_out=row_max[:, h:h + 1]).then_inc(scores_read, 1)
                dve.wait_ge(scores_read, LONG0 + n + 1)
                step(dve.scalar_tensor_tensor(weights[h % 2][:, :], weights[h % 2][:, :], SLOPE, weights[h % 2][:, :],
                                              ALU.mult, ALU.max))
                step(dve.scalar_tensor_tensor(row_lrelu[:, h:h + 1], row_max[:, h:h + 1], SLOPE,
                                              row_max[:, h:h + 1], ALU.mult, ALU.max))
                dve.tensor_scalar(neg_max[:, h:h + 1], row_lrelu[:, h:h + 1], -SCALE, None, ALU.mult
                                  ).then_inc(neg_max_ready, 1)

            def long_copy(q, h):
                n = HEADS * q + h
                for k in range(2):
                    dve.wait_ge(weights_transposed, 3 * n + k + 1)
                    dve.wait_ge(long_out_ready, LONG0 + n)
                    dve.tensor_copy(weightsT[:, 4 * k:4 * k + 4, :],
                                    ring[:, k, :].rearrange("p (c n) -> p c n", c=4)).then_inc(weightsT_by_dve, 1)

            def long_tile(b, q):
                step = chain(dve, long_step, STEPS_LONG * q)
                dve.wait_ge(long_loaded, 32 * (q + 1))
                step(dve.tensor_scalar(long_adj[:, :], long_adj[:, :], 1.0, BIG, ALU.subtract, ALU.mult))
                long_max(step, q, 0)
                for h in range(HEADS):
                    if h + 1 < HEADS:
                        long_max(step, q, h + 1)
                    long_copy(q, h)
                dve.wait_ge(long_out_ready, LONG0 + HEADS * (q + 1))
                step(dve.reciprocal(row_rcp[:, :], row_sum[:, :]))
                la = long_a[:, 0, :]
                step(dve.tensor_tensor(la.rearrange("p (h o) -> p h o", h=HEADS),
                                       long_out.rearrange("p (h o) -> p h o", h=HEADS),
                                       row_rcp[:, :].unsqueeze(2).broadcast_to([P, HEADS, OUT]), ALU.mult))
                step(dve.tensor_tensor(la, la, bias_bc[:, :], ALU.add))
                step(dve.scalar_tensor_tensor(la, la, 0.0, long_x[:, :], ALU.max, ALU.add))
                step(dve.tensor_reduce(long_stat[:, 0:1], la, X, ALU.add))
                step(dve.tensor_scalar(long_stat[:, 0:1], long_stat[:, 0:1], 1.0 / F, None, ALU.mult))
                dve.tensor_scalar(long_b[:, 0, :], la, long_stat[:, 0:1], None, ALU.subtract).then_inc(long_centred, 1)
                dve.wait_ge(long_squared, q + 1)
                step(dve.tensor_reduce(long_stat[:, 1:2], long_sq[:, 0, :], X, ALU.add))
                dve.tensor_scalar(long_stat[:, 1:2], long_stat[:, 1:2], 1.0 / F, EPS, ALU.mult, ALU.add
                                  ).then_inc(long_var, 1)
                dve.wait_ge(long_std, q + 1)
                step(dve.reciprocal(long_stat[:, 3:4], long_stat[:, 2:3]))
                dve.tensor_scalar(long_x1[:, :], long_b[:, 0, :], long_stat[:, 3:4], None, ALU.mult
                                  ).then_inc(long_x1_ready, 1)
                assert step.count() == STEPS_LONG

            def over_features(v, tiles=T):
                return v.unsqueeze(2).broadcast_to([P, tiles, F])

            def centre(step, t0, t1):
                step(dve.tensor_reduce(stat[:, 0, t0:t1], u[:, t0:t1, :], X, ALU.add))
                step(dve.tensor_scalar(stat[:, 0, t0:t1], stat[:, 0, t0:t1], 1.0 / F, None, ALU.mult))
                dve.tensor_tensor(uc[:, t0:t1, :], u[:, t0:t1, :], over_features(stat[:, 0, t0:t1], t1 - t0),
                                  ALU.subtract).then_inc(centred, 1)

            def variance(step, n, t0, t1):
                dve.wait_ge(squared, n)
                step(dve.tensor_reduce(stat[:, 1, t0:t1], sq[:, t0:t1, :], X, ALU.add))
                dve.tensor_scalar(stat[:, 1, t0:t1], stat[:, 1, t0:t1], 1.0 / F, EPS, ALU.mult, ALU.add
                                  ).then_inc(var_ready, 1)

            def reciprocal_std(step, n, t0, t1):
                dve.wait_ge(std_ready, n)
                step(dve.reciprocal(stat[:, 3, t0:t1], stat[:, 2, t0:t1]))

            S, SM = TS * HEADS, AS * HEADS

            def short(v, order="p t s h"):
                return v[:, 0:S].rearrange("p (t s h) -> " + order, t=T, s=SLOTS)

            def medium(v, order="p s h"):
                return v[:, S:SM].rearrange("p (s h) -> " + order, h=HEADS)

            def per_tile(v):
                return v[:, 0:T * HEADS].rearrange("p (t h) -> p t h", t=T)

            def attend_short_products(b):
                step = chain(dve, short_step, b.j)
                dve.wait_ge(proj_ready, (T // 2) * (b.j + 1))
                dve.wait_ge(slots_loaded[b.p], 16 * TS * (b.r + 1))
                step(dve.tensor_tensor(prod[:, 0:TS * F].rearrange("p (t s f) -> p t s f", t=T, s=SLOTS),
                                       gathered[b.p][:, :, :, 0:F],
                                       proj[b.p][:, 0:T, 0:F].unsqueeze(2).broadcast_to([P, T, SLOTS, F]), ALU.mult))

            def attend_short_sums(b):
                dve.tensor_reduce(score[:, 0:S], prod[:, 0:TS * F].rearrange("p (a d) -> p a d", d=ATT), X, ALU.add)

            def attend_medium_scores(b, step):
                dve.wait_ge(medium_slots_loaded, 16 * MSLOTS * (b.j + 1))
                dve.wait_ge(medium_rows_loaded, 32 * (b.j + 1))
                step(dve.tensor_tensor(prod[:, TS * F:AS * F].rearrange("p (s f) -> p s f", f=F),
                                       medium_gathered[:, :, 0:F],
                                       proj[b.p][:, T, 0:F].unsqueeze(1).broadcast_to([P, MSLOTS, F]), ALU.mult))
                step(dve.tensor_reduce(score[:, S:SM], prod[:, TS * F:AS * F].rearrange("p (a d) -> p a d", d=ATT),
                                       X, ALU.add))

            def attend_softmax(b, step):
                slot_head = score[:, :].rearrange("p (a h) -> p a h", h=HEADS)
                per_slot = penalty[b.p][:, :].unsqueeze(2).broadcast_to([P, AS, HEADS])
                step(dve.tensor_tensor(slot_head, slot_head, per_slot, ALU.add))
                step(dve.scalar_tensor_tensor(lrelu[:, :], score[:, :], SLOPE, score[:, :], ALU.mult, ALU.max))
                dve.tensor_reduce(per_tile(slot_max), short(lrelu, "p t h s"), X, ALU.max)
                step(dve.tensor_reduce(slot_max[:, T * HEADS:], medium(lrelu, "p h s"), X, ALU.max))
                dve.tensor_tensor(short(score), short(lrelu),
                                  per_tile(slot_max).unsqueeze(2).broadcast_to([P, T, SLOTS, HEADS]), ALU.subtract)
                dve.tensor_tensor(medium(score), medium(lrelu),
                                  slot_max[:, T * HEADS:].unsqueeze(1).broadcast_to([P, MSLOTS, HEADS]), ALU.subtract
                                  ).then_inc(exp_in_ready, 1)

            def attend_weights(b, step):
                G, M = gathered[b.p], medium_gathered
                dve.wait_ge(exp_ready, b.j + 1)
                dve.tensor_reduce(per_tile(den), short(expw, "p t h s"), X, ALU.add)
                step(dve.tensor_reduce(den[:, T * HEADS:], medium(expw, "p h s"), X, ALU.add))
                slot_head = expw[:, :].rearrange("p (a h) -> p a h", h=HEADS)
                per_slot = valid[b.p][:, :].unsqueeze(2).broadcast_to([P, AS, HEADS])
                step(dve.tensor_tensor(slot_head, slot_head, per_slot, ALU.mult))
                by_head = prod[:, 0:AS * F].rearrange("p (a h o) -> p a h o", h=HEADS, o=OUT)
                dve.tensor_tensor(by_head[:, 0:TS], G[:, :, :, F:2 * F].rearrange("p t s (h o) -> p (t s) h o", h=HEADS),
                                  slot_head[:, 0:TS].unsqueeze(3).broadcast_to([P, TS, HEADS, OUT]), ALU.mult)
                dve.tensor_tensor(by_head[:, TS:AS], M[:, :, F:2 * F].rearrange("p s (h o) -> p s h o", h=HEADS),
                                  slot_head[:, TS:AS].unsqueeze(3).broadcast_to([P, MSLOTS, HEADS, OUT]), ALU.mult
                                  ).then_inc(gathered_read, 1)
                dve.wait_ge(gathered_read, ATTEND0 + b.j + 1)

            def attend_sums(b, step):
                dve.tensor_reduce(u[:, 0:T, :], prod[:, 0:TS * F].rearrange("p (t s f) -> p t f s", t=T, s=SLOTS),
                                  X, ALU.add)
                step(dve.tensor_reduce(u[:, T, :], prod[:, TS * F:AS * F].rearrange("p (s f) -> p f s", f=F),
                                       X, ALU.add))

            def attend_residual(b, step):
                step(dve.reciprocal(den[:, :], den[:, :]))
                flat = u[:, :, :].rearrange("p t (h o) -> p (t h) o", h=HEADS)
                step(dve.tensor_tensor(flat, flat, den[:, :].unsqueeze(2).broadcast_to([P, (T + 1) * HEADS, OUT]),
                                       ALU.mult))
                step(dve.tensor_tensor(u[:, :, :], u[:, :, :], bias_bc[:, :].unsqueeze(1).broadcast_to([P, T + 1, HO]),
                                       ALU.add))
                step(dve.scalar_tensor_tensor(u[:, :, :], u[:, :, :], 0.0, x_in[b.p][:, :, :], ALU.max, ALU.add))

            def attend_x1(b, step):
                reciprocal_std(step, 2 * b.j + 1, 0, T + 1)
                dve.tensor_scalar(x1[:, T, :], uc[:, T, :], stat[:, 3, T:T + 1], None, ALU.mult
                                  ).then_inc(medium_x1_ready, 1)
                step(dve.tensor_tensor(x1[:, 0:T, :], uc[:, 0:T, :], over_features(stat[:, 3, 0:T]), ALU.mult))

            def merge(b):
                dve.wait_ge(merged_loaded[b.p], 16 * (b.r + 1))
                alone(dve)
                for t0, t1 in HALVES:
                    dve.copy_predicated(x1[:, t0:t1, :], over_features(is_long[b.p][:, t0:t1].bitcast(U32), t1 - t0),
                                        merged[:, t0:t1, :]).then_inc(part_in_ready, 1)
                for i, (t0, t1) in enumerate(HALVES):
                    dve.wait_ge(part_ready, 4 * b.j + i + 1)
                    dve.tensor_tensor(u[:, t0:t1, :], x1[:, t0:t1, :], x1_parts[:, t0:t1, 0, :], ALU.subtract
                                      ).then_inc(part_in_ready, 1)
                for i, (t0, t1) in enumerate(HALVES):
                    dve.wait_ge(part_ready, 4 * b.j + i + 3)
                    dve.tensor_tensor(x1_parts[:, t0:t1, 2, :], u[:, t0:t1, :], x1_parts[:, t0:t1, 1, :],
                                      ALU.subtract).then_inc(parts_ready, 1)

            def aggregate(b, groups):
                for g in groups:
                    dve.wait_ge(agg_ps_ready, AGG0 + (T // 2) * b.j + g + 1)
                    parts = mid[:, g % 3, :].rearrange("p (t c) -> p t c", t=2)[:, :, 0:3 * F]
                    dve.tensor_reduce(messages[:, 2 * g:2 * g + 2, :], parts.rearrange("p t (a f) -> p t f a", a=3),
                                      X, ALU.add).then_inc(agg_read, 1)

            def finish(b, step):
                dve.wait_ge(message_ready, T * (b.j + 1))
                step(dve.tensor_tensor(u[:, 0:T, :], messages, x1[:, 0:T, :], ALU.add))
                centre(step, 0, T)

            def finish_y(b, step):
                reciprocal_std(step, 2 * b.j + 2, 0, T)
                dve.tensor_tensor(y, y, over_features(stat[:, 3, 0:T], T), ALU.mult).then_inc(y_ready, 1)

            def dense(b):
                with dve.If(load_dense_tiles(dve, b) > 0):
                    first, end, batches = load_span(dve, b)
                    prepare_dense(b, batches)
                    alone(dve)
                    with dve.Fori(first, end) as q:
                        dve.wait_ge(dense_tile_over, LONG0 + q)
                        make_onehot(b, dense_list)
                        read_list(b, dense_list, q + 1, dense_load, dense_store)
                        step = chain(dve, rank_moved, q)
                        step(dve.tensor_scalar(rank[b.p][:, :], rank[b.p][:, :], float(P), None, ALU.subtract))
                        long_tile(b, q)

            def first_keys(b):
                step = chain(dve, first_step, STEPS_FIRST * b.j)
                step(dve.tensor_scalar(first_row[:, b.p:b.p + 1], first_row[:, b.p:b.p + 1], 2.0 * N, None, ALU.add))
                take_keys(b, 0, step)
                assert step.count() == STEPS_FIRST

            def period(b, next_b, after_next):
                dense(b)
                attend = chain(dve, attend_step, STEPS_ATTEND * b.j)
                agg = chain(dve, agg_step, STEPS_AGG * b.j)
                if next_b:
                    extract = chain(dve, extract_step, STEPS_EXTRACT * next_b.j)
                attend_medium_scores(b, attend)
                attend_softmax(b, attend)
                attend_weights(b, attend)
                if next_b:
                    take_keys(next_b, 1, extract)
                attend_sums(b, attend)
                if next_b:
                    take_keys(next_b, 2, extract)
                attend_residual(b, attend)
                if next_b:
                    take_keys(next_b, 3, extract)
                    kinds(next_b, extract)
                dve.wait_ge(y_stored, Y0 + 48 * b.j)
                centre(attend, 0, T + 1)
                if next_b:
                    medium_ranks(next_b, extract)
                variance(attend, 2 * b.j + 1, 0, T + 1)
                if next_b:
                    medium_rows(next_b)
                    assert extract.count() == STEPS_EXTRACT
                attend_x1(b, attend)
                assert attend.count() == STEPS_ATTEND
                agg(dve.tensor_scalar(inv_degree[:, :], degree[b.p][:, :], 1.0, None, ALU.max))
                agg(dve.reciprocal(inv_degree[:, :], inv_degree[:, :]))
                if next_b:
                    medium_chain = chain(dve, medium_step, STEPS_MEDIUM * next_b.j)
                    extract_medium(next_b, medium_chain)
                merge(b)
                if next_b:
                    extract_more(next_b, medium_chain)
                aggregate(b, range(0, 2))
                if next_b:
                    dense_tiles(next_b)
                aggregate(b, range(2, 4))
                if next_b:
                    attend_short_products(next_b)
                aggregate(b, range(4, T // 2))
                if next_b:
                    attend_short_sums(next_b)
                finish(b, agg)
                if after_next:
                    first_keys(after_next)
                variance(agg, 2 * b.j + 2, 0, T)
                finish_y(b, agg)
                assert agg.count() == STEPS_AGG

            batch0, batch1 = Batch(0, 0, 0), Batch(1, 1, 0)
            first_keys(batch0)
            extract = chain(dve, extract_step, 0)
            for g in range(1, GROUPS):
                take_keys(batch0, g, extract)
            kinds(batch0, extract)
            medium_ranks(batch0, extract)
            medium_rows(batch0)
            medium_chain = chain(dve, medium_step, 0)
            extract_medium(batch0, medium_chain)
            extract_more(batch0, medium_chain)
            dense_tiles(batch0)
            first_keys(batch1)
            attend_short_products(batch0)
            attend_short_sums(batch0)
            pipeline(period, dve)


_INS = ['x', 'adj', 'L0_gnn_kernel', 'L0_gnn_attention_kernel', 'L0_gnn_attention_kernel_2', 'L0_gnn_bias']


def kernel(**inputs):
    import numpy as _np
    import concourse.bacc as _bacc
    from concourse import mybir as _mybir
    from concourse.bass_utils import run_bass_kernel_spmd as _run

    nc = _bacc.Bacc("TRN2", target_bir_lowering=False, num_devices=1)
    arrays, args = {}, []
    for name in _INS:
        a = _np.ascontiguousarray(inputs[name])
        arrays[f"in_{name}_dram"] = a
        args.append(nc.dram_tensor(f"in_{name}_dram", a.shape, _mybir.dt.from_np(a.dtype), kind="ExternalInput").ap())
    args.append(nc.dram_tensor("out_0_dram", inputs["x"].shape, _mybir.dt.float32, kind="ExternalOutput").ap())
    gat_resnorm_kernel(nc, *args)
    r = _run(nc, [arrays], core_ids=[0])
    return r.results[0]["out_0_dram"]
```
